# Optimizing a Trainium2 kernel written in Bass

```python
import numpy as np
import jax
import jax.numpy as jnp

def _softmax(x, axis=-1):
    return jax.nn.softmax(x, axis=axis)

def _gelu(x):
    return jax.nn.gelu(x, approximate=True)

def _silu(x):
    return jax.nn.silu(x)

def _sigmoid(x):
    return jax.nn.sigmoid(x)

def _layernorm(x, axis=-1, eps=1e-05):
    m = jnp.mean(x, axis=axis, keepdims=True)
    v = jnp.var(x, axis=axis, keepdims=True)
    return (x - m) / jnp.sqrt(v + eps)

def _scatter_add(tgt, idx, src, axis=0):
    return tgt.at[idx].add(src)

def _segment_sum(src, seg, n):
    return jax.ops.segment_sum(src, seg, n)
kernel_name = 'mk_xattn_seq_d2_seqx_r8_e20281'

def setup_inputs(seed: int=0):
    np.random.seed(seed)
    _w = jnp.asarray

    def _rec_inputs():
        import jax
        import jax.numpy as jnp
        _rk = jax.random.key(seed)
        x = 7.22e-05 + 1 * jax.random.normal(jax.random.fold_in(_rk, 1), (4, 256, 128), jnp.float32)
        _lenS = 256 - jax.random.randint(jax.random.fold_in(_rk, 7), (4,), 0, max(1, 256 // 4) + 1, jnp.int32)
        _lenS2 = 256 - jax.random.randint(jax.random.fold_in(_rk, 8), (4,), 0, max(1, 256 // 4) + 1, jnp.int32)
        _ctx_768P = jax.random.normal(jax.random.fold_in(_rk, 11), (4, 16, 96), jnp.float32)
        _ctx_768c = jax.random.dirichlet(jax.random.fold_in(_rk, 511), 0.3 * jnp.ones((16,), jnp.float32), (4, 256))
        _ctx_768t = jnp.einsum('bsk,bkd->bsd', _ctx_768c, _ctx_768P)
        _ctx_768t = _ctx_768t * jax.lax.rsqrt(jnp.mean(jnp.square(_ctx_768t)) + 1e-12) * 0.953939
        ctx_768 = 0.00272024 + 0.999456 * (_ctx_768t + 0.3 * jax.random.normal(jax.random.fold_in(_rk, 611), (4, 256, 96), jnp.float32))
        return (x, ctx_768)
    x, ctx_768 = _rec_inputs()

    def _L0_xattn_setup():
        import jax, jax.numpy as jnp
        import numpy as np
        N_HEADS = 16
        D_HEAD = 64
        D_MODEL = 128
        D_COND = 96
        D_FF = 4 * D_MODEL
        EPS = 1e-05

        def _layernorm(x, g, b):
            m = jnp.mean(x, axis=-1, keepdims=True)
            v = jnp.mean(jnp.square(x - m), axis=-1, keepdims=True)
            return (x - m) * jax.lax.rsqrt(v + EPS) * g + b

        def _attention(x, cond, wq, wk, wv, wo, bo):
            B, Sq, _ = x.shape
            Sk = cond.shape[1]
            q = (x @ wq).reshape(B, Sq, N_HEADS, D_HEAD)
            k = (cond @ wk).reshape(B, Sk, N_HEADS, D_HEAD)
            v = (cond @ wv).reshape(B, Sk, N_HEADS, D_HEAD)
            scale = D_HEAD ** (-0.5)
            attn = jnp.einsum('bqhd,bkhd->bhqk', q, k) * scale
            attn = jax.nn.softmax(attn, axis=-1)
            out = jnp.einsum('bhqk,bkhd->bqhd', attn, v).reshape(B, Sq, N_HEADS * D_HEAD)
            return out @ wo + bo
        key = jax.random.key(seed)
        ks = jax.random.split(key, 16)
        d_attn = N_HEADS * D_HEAD
        s = lambda fan_in: fan_in ** (-0.5)
        inp = {'x': jax.random.normal(ks[0], (8, 128, D_MODEL), jnp.float32), 'cond': jax.random.normal(ks[1], (8, 77, D_COND), jnp.float32), 'wq1': jax.random.normal(ks[2], (D_MODEL, d_attn), jnp.float32) * s(D_MODEL), 'wk1': jax.random.normal(ks[3], (D_MODEL, d_attn), jnp.float32) * s(D_MODEL), 'wv1': jax.random.normal(ks[4], (D_MODEL, d_attn), jnp.float32) * s(D_MODEL), 'wo1': jax.random.normal(ks[5], (d_attn, D_MODEL), jnp.float32) * s(d_attn), 'bo1': jnp.zeros((D_MODEL,), jnp.float32), 'g1': jnp.ones((D_MODEL,), jnp.float32), 'b1': jnp.zeros((D_MODEL,), jnp.float32), 'wq2': jax.random.normal(ks[6], (D_MODEL, d_attn), jnp.float32) * s(D_MODEL), 'wk2': jax.random.normal(ks[7], (D_COND, d_attn), jnp.float32) * s(D_COND), 'wv2': jax.random.normal(ks[8], (D_COND, d_attn), jnp.float32) * s(D_COND), 'wo2': jax.random.normal(ks[9], (d_attn, D_MODEL), jnp.float32) * s(d_attn), 'bo2': jnp.zeros((D_MODEL,), jnp.float32), 'g2': jnp.ones((D_MODEL,), jnp.float32), 'b2': jnp.zeros((D_MODEL,), jnp.float32), 'w_ff1': jax.random.normal(ks[10], (D_MODEL, 2 * D_FF), jnp.float32) * s(D_MODEL), 'b_ff1': jnp.zeros((2 * D_FF,), jnp.float32), 'w_ff2': jax.random.normal(ks[11], (D_FF, D_MODEL), jnp.float32) * s(D_FF), 'b_ff2': jnp.zeros((D_MODEL,), jnp.float32), 'g3': jnp.ones((D_MODEL,), jnp.float32), 'b3': jnp.zeros((D_MODEL,), jnp.float32)}
        return inp
    _L0_xattn_all = _L0_xattn_setup()
    _L0_xattn_in = {k: v for k, v in _L0_xattn_all.items() if k in ('wq1', 'wk1', 'wv1', 'wo1', 'bo1', 'g1', 'b1', 'wq2', 'wk2', 'wv2', 'wo2', 'bo2', 'g2', 'b2', 'w_ff1', 'b_ff1', 'w_ff2', 'b_ff2', 'g3', 'b3')}
    del _L0_xattn_all

    def _L1_xattn_setup():
        import jax, jax.numpy as jnp
        import numpy as np
        DIM, HEADS, DHEAD, CTX_DIM = (128, 16, 64, 96)
        INNER = HEADS * DHEAD
        FF_HID = 4 * DIM
        EPS = 1e-05

        def _ln(x, g, b):
            mu = jnp.mean(x, axis=-1, keepdims=True)
            var = jnp.mean(jnp.square(x - mu), axis=-1, keepdims=True)
            return (x - mu) * jax.lax.rsqrt(var + EPS) * g + b

        def _attn(x, ctx, Wq, Wk, Wv, Wo, bo):
            b, n, _ = x.shape
            m = ctx.shape[1]
            q = (x @ Wq).reshape(b, n, HEADS, DHEAD)
            k = (ctx @ Wk).reshape(b, m, HEADS, DHEAD)
            v = (ctx @ Wv).reshape(b, m, HEADS, DHEAD)
            scale = DHEAD ** (-0.5)
            sim = jnp.einsum('bihd,bjhd->bhij', q, k) * scale
            attn = jax.nn.softmax(sim, axis=-1)
            out = jnp.einsum('bhij,bjhd->bihd', attn, v).reshape(b, n, INNER)
            return out @ Wo + bo
        key = jax.random.key(seed)
        ks = jax.random.split(key, 24)

        def w(k, shape, fan_in):
            return jax.random.normal(k, shape, jnp.float32) * fan_in ** (-0.5)
        inp = {'x': jax.random.normal(ks[0], (2, 256, DIM), jnp.float32), 'context': jax.random.normal(ks[1], (2, 77, CTX_DIM), jnp.float32), 'Wq1': w(ks[2], (DIM, INNER), DIM), 'Wk1': w(ks[3], (DIM, INNER), DIM), 'Wv1': w(ks[4], (DIM, INNER), DIM), 'Wo1': w(ks[5], (INNER, DIM), INNER), 'bo1': jnp.zeros((DIM,), jnp.float32), 'Wq2': w(ks[6], (DIM, INNER), DIM), 'Wk2': w(ks[7], (CTX_DIM, INNER), CTX_DIM), 'Wv2': w(ks[8], (CTX_DIM, INNER), CTX_DIM), 'Wo2': w(ks[9], (INNER, DIM), INNER), 'bo2': jnp.zeros((DIM,), jnp.float32), 'Wp': w(ks[10], (DIM, 2 * FF_HID), DIM), 'bp': jnp.zeros((2 * FF_HID,), jnp.float32), 'W2': w(ks[11], (FF_HID, DIM), FF_HID), 'b2': jnp.zeros((DIM,), jnp.float32), 'g1': jnp.ones((DIM,), jnp.float32), 'be1': jnp.zeros((DIM,), jnp.float32), 'g2': jnp.ones((DIM,), jnp.float32), 'be2': jnp.zeros((DIM,), jnp.float32), 'g3': jnp.ones((DIM,), jnp.float32), 'be3': jnp.zeros((DIM,), jnp.float32)}
        return inp
    _L1_xattn_all = _L1_xattn_setup()
    _L1_xattn_in = {k: v for k, v in _L1_xattn_all.items() if k in ('Wq1', 'Wk1', 'Wv1', 'Wo1', 'bo1', 'Wq2', 'Wk2', 'Wv2', 'Wo2', 'bo2', 'Wp', 'bp', 'W2', 'b2', 'g1', 'be1', 'g2', 'be2', 'g3', 'be3')}
    del _L1_xattn_all
    return {'x': x, 'ctx_768': ctx_768, 'L0_xattn_wq1': _L0_xattn_in['wq1'], 'L0_xattn_wk1': _L0_xattn_in['wk1'], 'L0_xattn_wv1': _L0_xattn_in['wv1'], 'L0_xattn_wo1': _L0_xattn_in['wo1'], 'L0_xattn_bo1': _L0_xattn_in['bo1'], 'L0_xattn_g1': _L0_xattn_in['g1'], 'L0_xattn_b1': _L0_xattn_in['b1'], 'L0_xattn_wq2': _L0_xattn_in['wq2'], 'L0_xattn_wk2': _L0_xattn_in['wk2'], 'L0_xattn_wv2': _L0_xattn_in['wv2'], 'L0_xattn_wo2': _L0_xattn_in['wo2'], 'L0_xattn_bo2': _L0_xattn_in['bo2'], 'L0_xattn_g2': _L0_xattn_in['g2'], 'L0_xattn_b2': _L0_xattn_in['b2'], 'L0_xattn_w_ff1': _L0_xattn_in['w_ff1'], 'L0_xattn_b_ff1': _L0_xattn_in['b_ff1'], 'L0_xattn_w_ff2': _L0_xattn_in['w_ff2'], 'L0_xattn_b_ff2': _L0_xattn_in['b_ff2'], 'L0_xattn_g3': _L0_xattn_in['g3'], 'L0_xattn_b3': _L0_xattn_in['b3'], 'L1_xattn_Wq1': _L1_xattn_in['Wq1'], 'L1_xattn_Wk1': _L1_xattn_in['Wk1'], 'L1_xattn_Wv1': _L1_xattn_in['Wv1'], 'L1_xattn_Wo1': _L1_xattn_in['Wo1'], 'L1_xattn_bo1': _L1_xattn_in['bo1'], 'L1_xattn_Wq2': _L1_xattn_in['Wq2'], 'L1_xattn_Wk2': _L1_xattn_in['Wk2'], 'L1_xattn_Wv2': _L1_xattn_in['Wv2'], 'L1_xattn_Wo2': _L1_xattn_in['Wo2'], 'L1_xattn_bo2': _L1_xattn_in['bo2'], 'L1_xattn_Wp': _L1_xattn_in['Wp'], 'L1_xattn_bp': _L1_xattn_in['bp'], 'L1_xattn_W2': _L1_xattn_in['W2'], 'L1_xattn_b2': _L1_xattn_in['b2'], 'L1_xattn_g1': _L1_xattn_in['g1'], 'L1_xattn_be1': _L1_xattn_in['be1'], 'L1_xattn_g2': _L1_xattn_in['g2'], 'L1_xattn_be2': _L1_xattn_in['be2'], 'L1_xattn_g3': _L1_xattn_in['g3'], 'L1_xattn_be3': _L1_xattn_in['be3']}

def reference(x, ctx_768, L0_xattn_wq1, L0_xattn_wk1, L0_xattn_wv1, L0_xattn_wo1, L0_xattn_bo1, L0_xattn_g1, L0_xattn_b1, L0_xattn_wq2, L0_xattn_wk2, L0_xattn_wv2, L0_xattn_wo2, L0_xattn_bo2, L0_xattn_g2, L0_xattn_b2, L0_xattn_w_ff1, L0_xattn_b_ff1, L0_xattn_w_ff2, L0_xattn_b_ff2, L0_xattn_g3, L0_xattn_b3, L1_xattn_Wq1, L1_xattn_Wk1, L1_xattn_Wv1, L1_xattn_Wo1, L1_xattn_bo1, L1_xattn_Wq2, L1_xattn_Wk2, L1_xattn_Wv2, L1_xattn_Wo2, L1_xattn_bo2, L1_xattn_Wp, L1_xattn_bp, L1_xattn_W2, L1_xattn_b2, L1_xattn_g1, L1_xattn_be1, L1_xattn_g2, L1_xattn_be2, L1_xattn_g3, L1_xattn_be3):
    import jax
    import jax.numpy as jnp

    def _L0_xattn_ref(x, cond, wq1, wk1, wv1, wo1, bo1, g1, b1, wq2, wk2, wv2, wo2, bo2, g2, b2, w_ff1, b_ff1, w_ff2, b_ff2, g3, b3):
        import jax, jax.numpy as jnp
        import numpy as np
        N_HEADS = 16
        D_HEAD = 64
        D_MODEL = 128
        D_COND = 96
        D_FF = 4 * D_MODEL
        EPS = 1e-05

        def _layernorm(x, g, b):
            m = jnp.mean(x, axis=-1, keepdims=True)
            v = jnp.mean(jnp.square(x - m), axis=-1, keepdims=True)
            return (x - m) * jax.lax.rsqrt(v + EPS) * g + b

        def _attention(x, cond, wq, wk, wv, wo, bo):
            B, Sq, _ = x.shape
            Sk = cond.shape[1]
            q = (x @ wq).reshape(B, Sq, N_HEADS, D_HEAD)
            k = (cond @ wk).reshape(B, Sk, N_HEADS, D_HEAD)
            v = (cond @ wv).reshape(B, Sk, N_HEADS, D_HEAD)
            scale = D_HEAD ** (-0.5)
            attn = jnp.einsum('bqhd,bkhd->bhqk', q, k) * scale
            attn = jax.nn.softmax(attn, axis=-1)
            out = jnp.einsum('bhqk,bkhd->bqhd', attn, v).reshape(B, Sq, N_HEADS * D_HEAD)
            return out @ wo + bo
        h = _layernorm(x, g1, b1)
        x = _attention(h, h, wq1, wk1, wv1, wo1, bo1) + x
        h = _layernorm(x, g2, b2)
        x = _attention(h, cond, wq2, wk2, wv2, wo2, bo2) + x
        h = _layernorm(x, g3, b3)
        proj = h @ w_ff1 + b_ff1
        a, gate = jnp.split(proj, 2, axis=-1)
        ff = a * jax.nn.gelu(gate, approximate=False) @ w_ff2 + b_ff2
        return ff + x

    def _L1_xattn_ref(x, context, Wq1, Wk1, Wv1, Wo1, bo1, Wq2, Wk2, Wv2, Wo2, bo2, Wp, bp, W2, b2, g1, be1, g2, be2, g3, be3):
        import jax, jax.numpy as jnp
        import numpy as np
        DIM, HEADS, DHEAD, CTX_DIM = (128, 16, 64, 96)
        INNER = HEADS * DHEAD
        FF_HID = 4 * DIM
        EPS = 1e-05

        def _ln(x, g, b):
            mu = jnp.mean(x, axis=-1, keepdims=True)
            var = jnp.mean(jnp.square(x - mu), axis=-1, keepdims=True)
            return (x - mu) * jax.lax.rsqrt(var + EPS) * g + b

        def _attn(x, ctx, Wq, Wk, Wv, Wo, bo):
            b, n, _ = x.shape
            m = ctx.shape[1]
            q = (x @ Wq).reshape(b, n, HEADS, DHEAD)
            k = (ctx @ Wk).reshape(b, m, HEADS, DHEAD)
            v = (ctx @ Wv).reshape(b, m, HEADS, DHEAD)
            scale = DHEAD ** (-0.5)
            sim = jnp.einsum('bihd,bjhd->bhij', q, k) * scale
            attn = jax.nn.softmax(sim, axis=-1)
            out = jnp.einsum('bhij,bjhd->bihd', attn, v).reshape(b, n, INNER)
            return out @ Wo + bo
        h = _ln(x, g1, be1)
        x = _attn(h, h, Wq1, Wk1, Wv1, Wo1, bo1) + x
        h = _ln(x, g2, be2)
        x = _attn(h, context, Wq2, Wk2, Wv2, Wo2, bo2) + x
        h = _ln(x, g3, be3)
        y = h @ Wp + bp
        a, gate = (y[..., :FF_HID], y[..., FF_HID:])
        x = a * jax.nn.gelu(gate, approximate=False) @ W2 + b2 + x
        return x
    x = _L0_xattn_ref(x, ctx_768, L0_xattn_wq1, L0_xattn_wk1, L0_xattn_wv1, L0_xattn_wo1, L0_xattn_bo1, L0_xattn_g1, L0_xattn_b1, L0_xattn_wq2, L0_xattn_wk2, L0_xattn_wv2, L0_xattn_wo2, L0_xattn_bo2, L0_xattn_g2, L0_xattn_b2, L0_xattn_w_ff1, L0_xattn_b_ff1, L0_xattn_w_ff2, L0_xattn_b_ff2, L0_xattn_g3, L0_xattn_b3)
    x = _L1_xattn_ref(x, ctx_768, L1_xattn_Wq1, L1_xattn_Wk1, L1_xattn_Wv1, L1_xattn_Wo1, L1_xattn_bo1, L1_xattn_Wq2, L1_xattn_Wk2, L1_xattn_Wv2, L1_xattn_Wo2, L1_xattn_bo2, L1_xattn_Wp, L1_xattn_bp, L1_xattn_W2, L1_xattn_b2, L1_xattn_g1, L1_xattn_be1, L1_xattn_g2, L1_xattn_be2, L1_xattn_g3, L1_xattn_be3)
    return x

_drawn_inputs = setup_inputs


def setup_inputs(seed=0):
    import zlib

    import numpy as np

    out = dict(_drawn_inputs(seed))
    spreads = {'L0_xattn_bo1': (0.0, 0.1),
     'L0_xattn_g1': (1.0, 0.2),
     'L0_xattn_b1': (0.0, 0.1),
     'L0_xattn_bo2': (0.0, 0.1),
     'L0_xattn_g2': (1.0, 0.2),
     'L0_xattn_b2': (0.0, 0.369),
     'L0_xattn_b_ff1': (0.0, 0.1),
     'L0_xattn_b_ff2': (0.0, 0.1),
     'L0_xattn_g3': (1.0, 0.2),
     'L0_xattn_b3': (0.0, 0.1),
     'L1_xattn_bo1': (0.0, 0.1),
     'L1_xattn_bo2': (0.0, 0.1),
     'L1_xattn_bp': (0.0, 0.1),
     'L1_xattn_b2': (0.0, 0.1),
     'L1_xattn_g1': (1.0, 0.2),
     'L1_xattn_be1': (0.0, 0.1),
     'L1_xattn_g2': (1.0, 0.6),
     'L1_xattn_be2': (0.0, 0.643),
     'L1_xattn_g3': (1.0, 0.2),
     'L1_xattn_be3': (0.0, 0.1)}
    factors = {}
    for name, (base, spread) in spreads.items():
        noise = np.random.default_rng([zlib.crc32(name.encode()), seed]).standard_normal(out[name].shape)
        drawn = base * np.exp(spread * noise) if base else spread * noise
        out[name] = jnp.asarray(drawn.astype(out[name].dtype))
    for name, factor in factors.items():
        out[name] = (out[name] * factor).astype(out[name].dtype)
    return out
```

```python
from contextlib import ExitStack

import concourse.bass as bass
from concourse import mybir

F32 = mybir.dt.float32
F32R = mybir.dt.float32r
I32 = mybir.dt.int32
ACT = mybir.ActivationFunctionType
ALU = mybir.AluOpType
AX = mybir.AxisListType

P = 128
EPS = 1e-5
RSQRT_MAGIC = 1597463007.0
NEWTON_STEPS = 3
LN_LINKS = 4 + 3 * NEWTON_STEPS + 3


def transformer_kernel(nc, x, ctx, wq, wk_self, wv_self, wk_cross, wv_cross, wo, w_up, w_down,
                       columns, rows, out):
    batches, seq, width = x.shape
    layers = w_up.shape[0]
    inner = wq.shape[2]
    ctx_width = ctx.shape[2]
    head_dim = 64
    pairs = inner // P
    tokens = batches * seq
    tiles = tokens // P
    halves = 2
    half = tokens // halves
    tiles_half = tiles // halves
    seq_tiles = seq // P
    units = batches * 2
    hidden = w_down.shape[1]
    hidden_tiles = hidden // P
    scale = float(head_dim) ** -0.5
    vcols = head_dim + 1
    heads_chunk = 512 // head_dim
    v_chunks = tiles * inner // 512
    n_cols = columns.shape[1] // layers
    G = {"self": 0, "cross": 2, "mlp": 4}
    B_UP = 6
    ROW = {"self": 0, "cross": 1, "mlp": 2}
    ATT = {"self": 0, "cross": 1}
    LN = {"self": 0, "cross": 1, "mlp": 2}
    assert width == P and seq == 256 and tokens == 1024 and units == 8 and pairs == 8

    with ExitStack() as stack:
        def sb(name, shape, dt=F32):
            return stack.enter_context(nc.sbuf_tensor(name, shape, dt))

        def sem(name):
            return stack.enter_context(nc.semaphore(name))

        def bank(name):
            return stack.enter_context(nc.psum_tensor(name, [P, 512], F32))

        ident = sb("ident", [P, P])
        cols = sb("cols", [P, layers * n_cols])
        rows_all = sb("rows_all", [P, layers * 3 * width])
        x_sb = sb("x_sb", [P, tiles, width])
        xn = sb("xn", [P, tiles, width])
        stats = sb("stats", [P, tiles, 6])
        mean_var = sb("mean_var", [P, tiles, 2])
        var_eps = sb("var_eps", [P, tiles])
        half_var = sb("half_var", [P, tiles])
        rstd = sb("rstd", [P, tiles])
        newton = sb("newton", [P, tiles])
        h_full = sb("h_full", [P, tokens])
        h_hi = sb("h_hi", [P, tokens], F32R)
        h_lo = sb("h_lo", [P, tokens], F32R)
        ctx_rows = sb("ctx_rows", [P, tiles, ctx_width])
        ctx_hi = sb("ctx_hi", [P, tokens], F32R)
        ctx_lo = sb("ctx_lo", [P, tokens], F32R)
        wq_raw = sb("wq_raw", [P, inner])
        wk_raw = sb("wk_raw", [P, inner])
        wv_raw = sb("wv_raw", [P, inner])
        wo_sb = sb("wo_sb", [P, pairs, width])
        w_down_sb = sb("w_down_sb", [P, hidden_tiles, width])
        wv_hi = sb("wv_hi", [P, inner], F32R)
        wv_lo = sb("wv_lo", [P, inner], F32R)
        wp_hi = sb("wp_hi", [P, 2, P], F32R)
        wp_lo = sb("wp_lo", [P, 2, P], F32R)
        w_up_raw = sb("w_up_raw", [P, 2 * hidden])
        w_up_hi = sb("w_up_hi", [P, 2 * hidden], F32R)
        w_up_lo = sb("w_up_lo", [P, 2 * hidden], F32R)
        qk_hi = [sb("q_hi", [P, tokens], F32R), sb("k_hi", [P, tokens], F32R)]
        qk_lo = [sb("q_lo", [P, tokens], F32R), sb("k_lo", [P, tokens], F32R)]
        v_sb = sb("v_sb", [P, tiles, inner // head_dim * vcols])
        neg_max = sb("neg_max", [P, 4, seq_tiles])
        probs = sb("probs", [P, 4, seq_tiles, seq])
        probs_t = sb("probs_t", [P, 2, seq_tiles, seq])
        inv_sum = sb("inv_sum", [P, 2, seq_tiles, 1])
        heads_out = sb("heads_out", [P, 2, seq_tiles, P])
        heads_t = sb("heads_t", [P, pairs, tokens])
        hidden_t = heads_t
        gate = sb("gate", [P, 2, half])
        credits = sb("credits", [P, 3])

        score_bank = [bank("score0"), bank("score1")]
        turn_bank = [bank("turn0"), bank("turn1")]
        pv_bank = [bank("pv0"), bank("pv1")]
        proj_bank = [bank("proj0"), bank("proj1")]

        x_loaded, ctx_loaded, cols_loaded, rows_loaded = (
            sem("x_loaded"), sem("ctx_loaded"), sem("cols_loaded"), sem("rows_loaded"))
        wv_loaded, wqk_loaded, wo_loaded = sem("wv_loaded"), sem("wqk_loaded"), sem("wo_loaded")
        w_up_loaded, w_down_loaded = sem("w_up_loaded"), sem("w_down_loaded")
        out_stored = sem("out_stored")
        zeroed, ident_ready, ones_ready = sem("zeroed"), sem("ident_ready"), sem("ones_ready")
        ctx_turned, ctx_hi_ready, ctx_ready = sem("ctx_turned"), sem("ctx_hi_ready"), sem("ctx_ready")
        wv_split, pair_split, w_up_split = sem("wv_split"), sem("pair_split"), sem("w_up_split")
        v_made, qk_made = sem("v_made"), sem("qk_made")
        wo_used, w_down_used = sem("wo_used"), sem("w_down_used")
        pool_link = sem("pool_link")
        row_added = sem("row_added")
        ln_link, ln_turned, h_ready = sem("ln_link"), sem("ln_turned"), sem("h_ready")
        v_out_act, v_out_dve = sem("v_out_act"), sem("v_out_dve")
        qk_hi_out, qk_lo_out = sem("qk_hi_out"), sem("qk_lo_out")
        scored, maxed, exped, turned = sem("scored"), sem("maxed"), sem("exped"), sem("turned")
        turned_out_dve, turned_out_act = sem("turned_out_dve"), sem("turned_out_act")
        pv_made, inverted, normed = sem("pv_made"), sem("inverted"), sem("normed")
        heads_turned, heads_out_done = sem("heads_turned"), sem("heads_out_done")
        attended, residual_done = sem("attended"), sem("residual_done")
        up_made, gate_made, gate_done, hidden_done = (
            sem("up_made"), sem("gate_made"), sem("gate_done"), sem("hidden_done"))
        down_made = sem("down_made")

        def att_n(L, kind):
            return L * 2 + ATT[kind]

        def pair_n(L, kind, i):
            return L * (2 * pairs) + (ATT[kind] * pairs + i)

        def ln_n(L, kind, c):
            return L * (3 * halves) + (LN[kind] * halves + c)

        def half_cols(c):
            return slice(c * half, (c + 1) * half)

        def half_tiles(c):
            return range(c * tiles_half, (c + 1) * tiles_half)

        pool_held, pe_held, act_held, dve_held = (
            sem("pool_held"), sem("pe_held"), sem("act_held"), sem("dve_held"))

        block = stack.enter_context(nc.Block())

        @block.sync
        def _(sp):
            sp.dma_start(x_sb[:], x.rearrange("b (t p) d -> p (b t) d", p=P)).then_inc(x_loaded, 16)
            sp.dma_start(cols[:], columns).then_inc(cols_loaded, 16)
            sp.dma_start(ctx_rows[:], ctx.rearrange("b (t p) d -> p (b t) d", p=P)).then_inc(ctx_loaded, 16)

            def load_attention(L, kind):
                k_rows = P if kind == "self" else ctx_width
                wk, wv = (wk_self, wv_self) if kind == "self" else (wk_cross, wv_cross)
                n = att_n(L, kind)
                sp.wait_ge(wv_split, n + 1)
                sp.dma_start(wv_raw[0:k_rows, :], wv[bass.ds(L, 1)].rearrange("a p n -> (a p) n")
                             ).then_inc(wv_loaded, 16)
                sp.wait_ge(pair_split, n * pairs + 1)
                sp.dma_start(wq_raw[:], wq[bass.ds(n, 1)].rearrange("a p n -> (a p) n")
                             ).then_inc(wqk_loaded, 16)
                sp.dma_start(wk_raw[0:k_rows, :], wk[bass.ds(L, 1)].rearrange("a p n -> (a p) n")
                             ).then_inc(wqk_loaded, 16)
                sp.wait_ge(wo_used, n * halves + 1)
                sp.dma_start(wo_sb[:], wo[bass.ds(n, 1)].rearrange("a (i p) n -> p (a i) n", p=P)
                             ).then_inc(wo_loaded, 16)

            with sp.Fori(0, layers) as L:
                load_attention(L, "self")
                sp.wait_ge(w_up_split, L + 1)
                sp.dma_start(w_up_raw[:], w_up[bass.ds(L, 1)].rearrange("a p n -> (a p) n")
                             ).then_inc(w_up_loaded, 16)
                sp.wait_ge(w_down_used, L * halves + 1)
                sp.dma_start(w_down_sb[:], w_down[bass.ds(L, 1)].rearrange("a (f p) n -> p (a f) n", p=P)
                             ).then_inc(w_down_loaded, 16)
                load_attention(L, "cross")

            sp.wait_ge(residual_done, layers * 3 * halves)
            sp.dma_start(out.rearrange("b (t p) d -> p (b t) d", p=P), x_sb[:]).then_inc(out_stored, 16)
            sp.wait_ge(out_stored, 16)

        @block.gpsimd
        def _(pool):
            pool.dma_start(rows_all[:], rows.rearrange("a n -> (a n)").partition_broadcast(P)
                           ).then_inc(rows_loaded, 16)
            pool.memset(ident[:], 0.0).then_inc(zeroed, 1)
            pool.wait_ge(zeroed, 1)
            pool.affine_select(out=ident[:], in_=ident[:], compare_op=ALU.not_equal, fill=1.0, base=0,
                               pattern=[[-1, P]], channel_multiplier=1).then_inc(ident_ready, 1)
            v_heads = v_sb[:].rearrange("p t (h c) -> p (t h) c", c=vcols)
            pool.memset(v_heads[:, :, head_dim:vcols], 1.0).then_inc(ones_ready, 1)
            for k, credit in enumerate((wv_split, pair_split, w_up_split)):
                pool.memset(credits[:, k:k + 1], 0.0).then_inc(credit, 1)

            def split(hi, lo, raw, link, done):
                pool.tensor_copy(hi, raw).then_inc(pool_link, 1)
                pool.wait_ge(pool_link, link)
                return pool.tensor_tensor(lo, raw, hi.bitcast(F32), ALU.subtract).then_inc(done, 1)

            links_att = 1 + 2 * pairs
            links_layer = 2 * links_att + 1

            def split_pair(L, kind, i):
                k_rows = P if kind == "self" else ctx_width
                link = L * links_layer + (ATT[kind] * links_att + 1) + i * 2
                pool.wait_ge(qk_made, pair_n(L, kind, i) * 4 + 1)
                pool.sem_inc(pool_held, 1)
                at = bass.ds(i * P, P)
                pool.tensor_copy(wp_hi[:, 0, :], wq_raw[:, at]).then_inc(pool_link, 1)
                pool.tensor_copy(wp_hi[0:k_rows, 1, :], wk_raw[0:k_rows, at]).then_inc(pool_link, 1)
                pool.wait_ge(pool_link, link + 2)
                pool.sem_inc(pool_held, 1)
                pool.tensor_tensor(wp_lo[:, 0, :], wq_raw[:, at], wp_hi[:, 0, :].bitcast(F32), ALU.subtract)
                pool.tensor_tensor(wp_lo[0:k_rows, 1, :], wk_raw[0:k_rows, at],
                                   wp_hi[0:k_rows, 1, :].bitcast(F32), ALU.subtract).then_inc(pair_split, 1)

            def add_row(L, kind, c):
                pool.wait_ge(ln_link, ln_n(L, kind, c) * LN_LINKS + LN_LINKS - 2)
                pool.sem_inc(pool_held, 1)
                row = rows_all[:, bass.ds(L * (3 * width) + ROW[kind] * width, width)]
                for t in half_tiles(c):
                    last = pool.tensor_tensor(x_sb[:, t, :], x_sb[:, t, :], row, ALU.add)
                last.then_inc(row_added, 1)

            def attention(L, kind):
                k_rows = P if kind == "self" else ctx_width
                n = att_n(L, kind)
                pool.wait_ge(wv_loaded, (n + 1) * 16)
                pool.wait_ge(v_made, n * v_chunks + 1)
                pool.sem_inc(pool_held, 1)
                split(wv_hi[0:k_rows, :], wv_lo[0:k_rows, :], wv_raw[0:k_rows, :],
                      L * links_layer + ATT[kind] * links_att + 1, wv_split)
                pool.wait_ge(wqk_loaded, (n + 1) * 32)
                split_pair(L, kind, 0)
                for c in range(halves):
                    add_row(L, kind, c)
                with pool.Fori(1, pairs) as i:
                    split_pair(L, kind, i)

            pool.wait_ge(rows_loaded, 16)
            with pool.Fori(0, layers) as L:
                attention(L, "self")
                attention(L, "cross")
                pool.wait_ge(w_up_loaded, (L + 1) * 16)
                pool.wait_ge(w_down_used, L * halves + 1)
                pool.sem_inc(pool_held, 1)
                split(w_up_hi[:], w_up_lo[:], w_up_raw[:], (L + 1) * links_layer, w_up_split)
                for c in range(halves):
                    add_row(L, "mlp", c)

        @block.tensor
        def _(pe):
            def product(out_ap, st, mv):
                nc.tensor.matmul(out_ap, st[1], mv[0], start=True, stop=False)
                nc.tensor.matmul(out_ap, st[0], mv[1], start=False, stop=False)
                return nc.tensor.matmul(out_ap, st[0], mv[0], start=False, stop=True)

            def turn_norm(L, kind, c):
                pe.wait_ge(ln_link, ln_n(L, kind, c) * LN_LINKS + LN_LINKS - 2)
                for j, t in enumerate(half_tiles(c)):
                    last = nc.tensor.transpose(proj_bank[c][:, j * P:(j + 1) * P], xn[:, t, :], ident[:])
                last.then_inc(ln_turned, 1)

            def project_v(L, kind, c):
                k_rows, s_hi, s_lo = (P, h_hi, h_lo) if kind == "self" else (ctx_width, ctx_hi, ctx_lo)
                n = att_n(L, kind)
                per = v_chunks // halves
                for j in range(c * per, (c + 1) * per):
                    t, part = j // 2, j % 2
                    if j >= 2:
                        pe.wait_ge((v_out_act, v_out_dve)[j % 2], n * (v_chunks // 2) + j // 2)
                    at, to = slice(t * P, (t + 1) * P), slice(part * 512, (part + 1) * 512)
                    product(turn_bank[j % 2][:],
                            (s_hi[0:k_rows, at], s_lo[0:k_rows, at]),
                            (wv_hi[0:k_rows, to], wv_lo[0:k_rows, to])).then_inc(v_made, 1)

            def project_qk(kind, which, c, to_bank):
                k_rows, s_hi, s_lo = (P, h_hi, h_lo) if which == 0 or kind == "self" else (ctx_width, ctx_hi, ctx_lo)
                at = half_cols(c)
                product(proj_bank[to_bank][:],
                        (wp_hi[0:k_rows, which, :], wp_lo[0:k_rows, which, :]),
                        (s_hi[0:k_rows, at], s_lo[0:k_rows, at])).then_inc(qk_made, 1)

            def pair_body(L, kind, i, last_pair):
                n = pair_n(L, kind, i)

                def score(u):
                    b, hh = u // 2, u % 2
                    if u == 0:
                        pe.wait_ge(qk_lo_out, n * 4 + 2)
                    if u == units // 2:
                        pe.wait_ge(qk_lo_out, n * 4 + 4)
                    if u >= 2:
                        pe.wait_ge(exped, n * units + u - 1)
                    head = slice(hh * head_dim, (hh + 1) * head_dim)
                    keys = slice(b * seq, (b + 1) * seq)
                    for s in range(seq_tiles):
                        qs = slice(b * seq + s * P, b * seq + (s + 1) * P)
                        m = product(score_bank[u % 2][:, s * seq:(s + 1) * seq],
                                    (qk_hi[0][head, qs], qk_lo[0][head, qs]),
                                    (qk_hi[1][head, keys], qk_lo[1][head, keys]))
                    m.then_inc(scored, 1)

                def turn(u):
                    pe.wait_ge(exped, n * units + u + 1)
                    for kt in range(seq_tiles):
                        for s in range(seq_tiles):
                            m = nc.tensor.transpose(
                                turn_bank[u % 2][:, kt * seq + s * P:kt * seq + (s + 1) * P],
                                probs[:, u % 4, s, kt * P:(kt + 1) * P], ident[:])
                    m.then_inc(turned, 1)

                def weigh(u):
                    b, hh = u // 2, u % 2
                    pe.wait_ge((turned_out_dve, turned_out_act)[u % 2], n * (units // 2) + u // 2 + 1)
                    if u >= 2:
                        pe.wait_ge(normed, n * units + u - 1)
                    for s in range(seq_tiles):
                        for kt in range(seq_tiles):
                            m = nc.tensor.matmul(
                                pv_bank[u % 2][:, s * vcols:(s + 1) * vcols],
                                probs_t[:, u % 2, kt, s * P:(s + 1) * P],
                                v_sb[:, b * seq_tiles + kt, bass.ds(i * (2 * vcols) + hh * vcols, vcols)],
                                start=(kt == 0), stop=(kt == seq_tiles - 1))
                    m.then_inc(pv_made, 1)

                def turn_heads(b, to_bank):
                    pe.wait_ge(normed, n * units + 2 * b + 2)
                    for s in range(seq_tiles):
                        m = nc.tensor.transpose(proj_bank[to_bank][:, s * P:(s + 1) * P],
                                                heads_out[:, b % 2, s, :], ident[:])
                    m.then_inc(heads_turned, 1)

                for u in range(units):
                    score(u)
                    if u >= 2:
                        turn(u - 2)
                    if u >= 3:
                        weigh(u - 3)
                    if u == 5:
                        turn_heads(0, 0)
                    if u == 7:
                        pe.wait_ge(heads_out_done, n * batches + 1)
                        turn_heads(1, 1)
                if last_pair:
                    turn(6)
                    weigh(5)
                    turn(7)
                    weigh(6)
                    pe.wait_ge(heads_out_done, n * batches + 1)
                    turn_heads(2, 0)
                    project_out(L, kind, 0, (0, 1))
                    weigh(7)
                    pe.wait_ge(heads_out_done, n * batches + 2)
                    turn_heads(3, 1)
                    project_out(L, kind, 0, (2, 3))
                    project_out(L, kind, 1, (4, 5, 6, 7))
                    return
                pe.wait_ge(pair_split, n + 3)
                pe.wait_ge(heads_out_done, n * batches + 1)
                project_qk(kind, 0, 0, 0)
                turn(6)
                weigh(5)
                pe.wait_ge(heads_out_done, n * batches + 2)
                project_qk(kind, 1, 0, 1)
                turn(7)
                weigh(6)
                pe.wait_ge(qk_lo_out, n * 4 + 5)
                turn_heads(2, 0)
                pe.wait_ge(qk_lo_out, n * 4 + 6)
                project_qk(kind, 0, 1, 1)
                weigh(7)
                pe.wait_ge(heads_out_done, n * batches + 3)
                project_qk(kind, 1, 1, 0)
                pe.wait_ge(qk_lo_out, n * 4 + 7)
                turn_heads(3, 1)

            def project_out(L, kind, c, some_tiles):
                if some_tiles[0] % tiles_half == 0:
                    pe.wait_ge(wo_loaded, (att_n(L, kind) + 1) * 16)
                done = some_tiles[-1] // seq_tiles + 1
                pe.wait_ge(heads_out_done, (pair_n(L, kind, pairs - 1)) * batches + done)
                for t in some_tiles:
                    j = t % tiles_half
                    for i in range(pairs):
                        m = nc.tensor.matmul(score_bank[c][:, j * P:(j + 1) * P],
                                             heads_t[:, i, t * P:(t + 1) * P], wo_sb[:, i, :],
                                             start=(i == 0), stop=(i == pairs - 1))
                if some_tiles[-1] % tiles_half == tiles_half - 1:
                    m.then_inc(wo_used, 1)

            def attention(L, kind):
                n = att_n(L, kind)
                turn_norm(L, kind, 0)
                pe.wait_ge(wv_split, n + 2)
                if kind == "self":
                    pe.wait_ge(h_ready, ln_n(L, kind, 0) + 1)
                project_v(L, kind, 0)
                turn_norm(L, kind, 1)
                pe.wait_ge(pair_split, n * pairs + 2)
                pe.wait_ge(h_ready, ln_n(L, kind, 0) + 1)
                project_qk(kind, 0, 0, 0)
                pe.wait_ge(h_ready, ln_n(L, kind, 1) + 1)
                project_qk(kind, 1, 0, 1)
                project_v(L, kind, 1)
                pe.wait_ge(qk_lo_out, n * (pairs * 4) + 1)
                project_qk(kind, 0, 1, 0)
                pe.wait_ge(qk_lo_out, n * (pairs * 4) + 2)
                project_qk(kind, 1, 1, 1)
                pe.wait_ge(v_out_act, (n + 1) * (v_chunks // 2))
                pe.wait_ge(v_out_dve, (n + 1) * (v_chunks // 2))
                pe.sem_inc(pe_held, 1)
                with pe.Fori(0, pairs - 1) as i:
                    pair_body(L, kind, i, False)
                pair_body(L, kind, pairs - 1, True)

            def mlp(L):
                n = L * (halves * hidden_tiles)
                turn_norm(L, "mlp", 0)
                pe.wait_ge(w_up_split, L + 2)
                for c in range(halves):
                    if c == 1:
                        turn_norm(L, "mlp", 1)
                    pe.wait_ge(h_ready, ln_n(L, "mlp", c) + 1)
                    for f in range(hidden_tiles):
                        j = c * hidden_tiles + f
                        for which, to in ((1, score_bank), (0, turn_bank)):
                            if which == 1 and c == 0 and f < 2:
                                pe.wait_ge(residual_done, L * (3 * halves) + halves + f + 1)
                            if j >= 2:
                                pe.wait_ge((hidden_done, gate_done)[which], n + j - 1)
                            at = slice(which * hidden + f * P, which * hidden + (f + 1) * P)
                            product(to[j % 2][:], (w_up_hi[:, at], w_up_lo[:, at]),
                                    (h_hi[:, half_cols(c)], h_lo[:, half_cols(c)])
                                    ).then_inc((up_made, gate_made)[which], 1)
                pe.wait_ge(w_down_loaded, (L + 1) * 16)
                for c in range(halves):
                    pe.wait_ge(hidden_done, n + (c + 1) * hidden_tiles)
                    for t in half_tiles(c):
                        j = t % tiles_half
                        for f in range(hidden_tiles):
                            m = nc.tensor.matmul(proj_bank[c][:, j * P:(j + 1) * P],
                                                 hidden_t[:, f, t * P:(t + 1) * P], w_down_sb[:, f, :],
                                                 start=(f == 0), stop=(f == hidden_tiles - 1))
                    m.then_inc(w_down_used, 1)

            pe.wait_ge(ident_ready, 1)
            pe.wait_ge(ctx_loaded, 16)
            for c in range(halves):
                for j, t in enumerate(half_tiles(c)):
                    m = nc.tensor.transpose(turn_bank[c][0:ctx_width, j * P:(j + 1) * P],
                                            ctx_rows[:, t, :], ident[:])
                m.then_inc(ctx_turned, 1)
            for credit in (v_made, qk_made, wo_used, w_down_used):
                nc.tensor.transpose(pv_bank[0][0:ctx_width, 0:P], ctx_rows[:, 0, :], ident[:]).then_inc(credit, 1)
            pe.wait_ge(ctx_ready, halves)
            pe.wait_ge(ones_ready, 1)
            with pe.Fori(0, layers) as L:
                attention(L, "self")
                attention(L, "cross")
                mlp(L)

        @block.scalar
        def _(act):
            def v_out(L, kind, c):
                n = att_n(L, kind)
                per = v_chunks // halves
                for j in range(c * per, (c + 1) * per, 2):
                    act.wait_ge(v_made, n * v_chunks + j + 2)
                    nc.scalar.activation(v_part(j), bank_heads(turn_bank[j % 2]), ACT.Copy).then_inc(v_out_act, 1)

            def qk_high(n, j, which, c, from_bank):
                act.wait_ge(qk_made, n * 4 + j + 2)
                nc.scalar.activation(qk_hi[which][:, half_cols(c)], proj_bank[from_bank][:], ACT.Copy,
                                     scale=(scale, 1.0)[which]).then_inc(qk_hi_out, 1)

            def pair_body(L, kind, i, last_pair):
                n = pair_n(L, kind, i)

                def exponentials(u):
                    act.wait_ge(maxed, n * units + u + 1)
                    for s in range(seq_tiles):
                        m = nc.scalar.activation(probs[:, u % 4, s, :], score_bank[u % 2][:, s * seq:(s + 1) * seq],
                                                 ACT.Exp, bias=neg_max[:, u % 4, s:s + 1])
                    m.then_inc(exped, 1)

                def turned_out(u):
                    act.wait_ge(turned, n * units + u + 1)
                    nc.scalar.activation(probs_t[:, 1, :, :].rearrange("p a b -> p (a b)"),
                                         turn_bank[1][:], ACT.Copy).then_inc(turned_out_act, 1)

                def heads_t_out(b, from_bank):
                    act.wait_ge(heads_turned, n * batches + b + 1)
                    act.sem_inc(act_held, 1)
                    nc.scalar.activation(heads_t[:, bass.ds(i, 1), b * seq:(b + 1) * seq].rearrange("p a b -> p (a b)"),
                                         proj_bank[from_bank][:, 0:seq], ACT.Copy).then_inc(heads_out_done, 1)

                for u in range(units):
                    if u >= 3 and u % 2 == 1:
                        turned_out(u - 2)
                    exponentials(u)
                    if u == 6:
                        heads_t_out(0, 0)
                if last_pair:
                    heads_t_out(1, 1)
                    turned_out(7)
                    heads_t_out(2, 0)
                    heads_t_out(3, 1)
                    return
                heads_t_out(1, 1)
                qk_high(n, 4, 0, 0, 0)
                qk_high(n, 5, 1, 0, 1)
                turned_out(7)
                heads_t_out(2, 0)
                qk_high(n, 6, 0, 1, 1)
                qk_high(n, 7, 1, 1, 0)
                heads_t_out(3, 1)

            def attention(L, kind):
                n = pair_n(L, kind, 0)
                v_out(L, kind, 0)
                qk_high(n, 0, 0, 0, 0)
                qk_high(n, 1, 1, 0, 1)
                v_out(L, kind, 1)
                qk_high(n, 2, 0, 1, 0)
                qk_high(n, 3, 1, 1, 1)
                with act.Fori(0, pairs - 1) as i:
                    pair_body(L, kind, i, False)
                pair_body(L, kind, pairs - 1, True)

            def bank_heads(b):
                return b[:].rearrange("p (h c) -> p h c", c=head_dim)

            def v_part(j):
                t, part = j // 2, j % 2
                v_heads = v_sb[:, t, :].rearrange("p (h c) -> p h c", c=vcols)
                return v_heads[:, part * heads_chunk:(part + 1) * heads_chunk, 0:head_dim]

            act.wait_ge(cols_loaded, 16)
            with act.Fori(0, layers) as L:
                attention(L, "self")
                attention(L, "cross")
                n = L * (halves * hidden_tiles)
                for j in range(halves * hidden_tiles):
                    f = j % hidden_tiles
                    act.wait_ge(gate_made, n + j + 1)
                    if j >= 2:
                        act.wait_ge(hidden_done, n + j - 1)
                    act.sem_inc(act_held, 1)
                    nc.scalar.activation(gate[:, j % 2, :], score_bank[j % 2][:], ACT.Gelu,
                                         bias=cols[:, bass.ds(L * n_cols + (B_UP + hidden_tiles + f), 1)]
                                         ).then_inc(gate_done, 1)

        @block.vector
        def _(dve):
            def bank_heads(b):
                return b[:].rearrange("p (h c) -> p h c", c=head_dim)

            def v_part(j):
                t, part = j // 2, j % 2
                v_heads = v_sb[:, t, :].rearrange("p (h c) -> p h c", c=vcols)
                return v_heads[:, part * heads_chunk:(part + 1) * heads_chunk, 0:head_dim]

            def norm_rows(L, kind, c):
                base = ln_n(L, kind, c) * LN_LINKS
                ts = half_tiles(c)
                h = slice(ts[0], ts[-1] + 1)
                for t in ts:
                    m = nc.vector.bn_stats(stats[:, t, :], x_sb[:, t, :])
                m.then_inc(ln_link, 1)
                dve.wait_ge(ln_link, base + 1)
                dve.sem_inc(dve_held, 1)
                for t in ts:
                    m = nc.vector.bn_aggr(mean_var[:, t, :], stats[:, t, :])
                m.then_inc(ln_link, 1)
                dve.wait_ge(ln_link, base + 2)
                nc.vector.tensor_scalar(half_var[:, h], mean_var[:, h, 1], -0.5, -0.5 * EPS, ALU.mult, ALU.add)
                nc.vector.tensor_scalar(var_eps[:, h], mean_var[:, h, 1], EPS, None, ALU.add).then_inc(ln_link, 1)
                dve.wait_ge(ln_link, base + 3)
                nc.vector.tensor_scalar(rstd[:, h].bitcast(I32), var_eps[:, h].bitcast(I32), -0.5, RSQRT_MAGIC,
                                        ALU.mult, ALU.add).then_inc(ln_link, 1)
                for k in range(NEWTON_STEPS):
                    dve.wait_ge(ln_link, base + 4 + 3 * k)
                    nc.vector.tensor_tensor(newton[:, h], rstd[:, h], rstd[:, h], ALU.mult).then_inc(ln_link, 1)
                    dve.wait_ge(ln_link, base + 5 + 3 * k)
                    nc.vector.tensor_tensor(newton[:, h], newton[:, h], half_var[:, h], ALU.mult).then_inc(ln_link, 1)
                    dve.wait_ge(ln_link, base + 6 + 3 * k)
                    nc.vector.scalar_tensor_tensor(out=rstd[:, h], in0=newton[:, h], scalar=1.5, in1=rstd[:, h],
                                                   op0=ALU.add, op1=ALU.mult).then_inc(ln_link, 1)
                dve.wait_ge(ln_link, base + LN_LINKS - 3)
                for t in ts:
                    m = nc.vector.tensor_scalar(xn[:, t, :], x_sb[:, t, :], mean_var[:, t, 0:1], rstd[:, t:t + 1],
                                                ALU.subtract, ALU.mult)
                m.then_inc(ln_link, 1)

            def norm_parts(L, kind, c):
                n = ln_n(L, kind, c)
                at = half_cols(c)
                dve.wait_ge(ln_turned, n + 1)
                nc.vector.tensor_scalar(h_full[:, at], proj_bank[c][:],
                                        cols[:, bass.ds(L * n_cols + G[kind], 1)],
                                        cols[:, bass.ds(L * n_cols + G[kind] + 1, 1)],
                                        ALU.mult, ALU.add).then_inc(ln_link, 1)
                dve.wait_ge(ln_link, n * LN_LINKS + LN_LINKS - 1)
                nc.vector.tensor_copy(h_hi[:, at], h_full[:, at]).then_inc(ln_link, 1)
                dve.wait_ge(ln_link, n * LN_LINKS + LN_LINKS)
                nc.vector.tensor_tensor(h_lo[:, at], h_full[:, at], h_hi[:, at].bitcast(F32),
                                        ALU.subtract).then_inc(h_ready, 1)

            def residual(L, stage, c, from_bank):
                n = L * (3 * halves) + LN[stage] * halves + c
                dve.wait_ge(row_added, n + 1)
                at = half_tiles(c)
                rows_c = x_sb[:, at[0]:at[-1] + 1, :].rearrange("p t d -> p (t d)")
                nc.vector.tensor_tensor(rows_c, from_bank[:], rows_c, ALU.add).then_inc(residual_done, 1)
                return n + 1

            def v_out(L, kind, c):
                n = att_n(L, kind)
                per = v_chunks // halves
                for j in range(c * per + 1, (c + 1) * per, 2):
                    dve.wait_ge(v_made, n * v_chunks + j + 2)
                    nc.vector.tensor_copy(v_part(j), bank_heads(turn_bank[j % 2])).then_inc(v_out_dve, 1)

            def qk_low(n, j, which, c, from_bank):
                dve.wait_ge(qk_hi_out, n * 4 + j + 1)
                nc.vector.scalar_tensor_tensor(out=qk_lo[which][:, half_cols(c)], in0=proj_bank[from_bank][:],
                                               scalar=(scale, 1.0)[which],
                                               in1=qk_hi[which][:, half_cols(c)].bitcast(F32),
                                               op0=ALU.mult, op1=ALU.subtract).then_inc(qk_lo_out, 1)

            def pair_body(L, kind, i, last_pair):
                n = pair_n(L, kind, i)

                def maxima(u):
                    dve.wait_ge(scored, n * units + u + 1)
                    nc.vector.tensor_reduce(neg_max[:, u % 4, :],
                                            score_bank[u % 2][:].rearrange("p (s k) -> p s k", k=seq),
                                            AX.X, ALU.max, negate=True).then_inc(maxed, 1)

                def turned_out(u):
                    dve.wait_ge(turned, n * units + u + 1)
                    nc.vector.tensor_copy(probs_t[:, 0, :, :].rearrange("p a b -> p (a b)"),
                                          turn_bank[0][:]).then_inc(turned_out_dve, 1)

                def normalise(u):
                    b, hh = u // 2, u % 2
                    dve.wait_ge(pv_made, n * units + u + 1)
                    weighed = pv_bank[u % 2][:, 0:seq_tiles * vcols].rearrange("p (s c) -> p s c", c=vcols)
                    nc.vector.reciprocal(inv_sum[:, u % 2, :, :], weighed[:, :, head_dim:vcols]).then_inc(inverted, 1)
                    dve.wait_ge(inverted, n * units + u + 1)
                    nc.vector.tensor_tensor(heads_out[:, b % 2, :, hh * head_dim:(hh + 1) * head_dim],
                                            weighed[:, :, 0:head_dim],
                                            inv_sum[:, u % 2, :, :].to_broadcast([P, seq_tiles, head_dim]),
                                            ALU.mult).then_inc(normed, 1)

                for u in range(units):
                    maxima(u)
                    if u >= 2 and u % 2 == 0:
                        turned_out(u - 2)
                    if u >= 3:
                        normalise(u - 3)
                if last_pair:
                    turned_out(6)
                    normalise(5)
                    normalise(6)
                    normalise(7)
                    return
                qk_low(n, 4, 0, 0, 0)
                turned_out(6)
                normalise(5)
                qk_low(n, 5, 1, 0, 1)
                normalise(6)
                qk_low(n, 6, 0, 1, 1)
                normalise(7)
                qk_low(n, 7, 1, 1, 0)

            def attention(L, kind):
                n = pair_n(L, kind, 0)
                norm_parts(L, kind, 0)
                if kind == "self":
                    norm_rows(L, kind, 1)
                    v_out(L, kind, 0)
                else:
                    sum_then_norm(L, "self", "cross", 1)
                    v_out(L, kind, 0)
                norm_parts(L, kind, 1)
                qk_low(n, 0, 0, 0, 0)
                qk_low(n, 1, 1, 0, 1)
                v_out(L, kind, 1)
                qk_low(n, 2, 0, 1, 0)
                qk_low(n, 3, 1, 1, 1)
                with dve.Fori(0, pairs - 1) as i:
                    pair_body(L, kind, i, False)
                pair_body(L, kind, pairs - 1, True)

            def sum_then_norm(L, stage, then, c):
                dve.wait_ge(wo_used, att_n(L, stage) * halves + c + 2)
                done = residual(L, stage, c, score_bank[c])
                dve.wait_ge(residual_done, done)
                norm_rows(L, then, c)

            dve.wait_ge(cols_loaded, 16)
            for c in range(halves):
                dve.wait_ge(ctx_turned, c + 1)
                at = half_cols(c)
                nc.vector.tensor_copy(ctx_hi[0:ctx_width, at], turn_bank[c][0:ctx_width, :]).then_inc(ctx_hi_ready, 1)
                dve.wait_ge(ctx_hi_ready, c + 1)
                nc.vector.tensor_tensor(ctx_lo[0:ctx_width, at], turn_bank[c][0:ctx_width, :],
                                        ctx_hi[0:ctx_width, at].bitcast(F32), ALU.subtract).then_inc(ctx_ready, 1)
            dve.wait_ge(x_loaded, 16)
            with dve.Fori(0, layers) as L:
                norm_rows(L, "self", 0)
                attention(L, "self")
                sum_then_norm(L, "self", "cross", 0)
                attention(L, "cross")
                sum_then_norm(L, "cross", "mlp", 0)
                norm_parts(L, "mlp", 0)
                sum_then_norm(L, "cross", "mlp", 1)
                n = L * (halves * hidden_tiles)
                for c in range(halves):
                    if c == 1:
                        norm_parts(L, "mlp", 1)
                    for f in range(hidden_tiles):
                        j = c * hidden_tiles + f
                        dve.wait_ge(up_made, n + j + 1)
                        dve.wait_ge(gate_done, n + j + 1)
                        nc.vector.scalar_tensor_tensor(out=hidden_t[:, f, half_cols(c)], in0=turn_bank[j % 2][:],
                                                       scalar=cols[:, bass.ds(L * n_cols + (B_UP + f), 1)],
                                                       in1=gate[:, j % 2, :],
                                                       op0=ALU.add, op1=ALU.mult).then_inc(hidden_done, 1)
                for c in range(halves):
                    dve.wait_ge(w_down_used, L * halves + c + 2)
                    done = residual(L, "mlp", c, proj_bank[c])
                dve.wait_ge(residual_done, done)


_NAMES = [
    {"wq": ("wq1", "wq2"), "wk": ("wk1", "wk2"), "wv": ("wv1", "wv2"), "wo": ("wo1", "wo2"),
     "bo": ("bo1", "bo2"), "g": ("g1", "g2", "g3"), "b": ("b1", "b2", "b3"),
     "w_up": "w_ff1", "b_up": "b_ff1", "w_down": "w_ff2", "b_down": "b_ff2"},
    {"wq": ("Wq1", "Wq2"), "wk": ("Wk1", "Wk2"), "wv": ("Wv1", "Wv2"), "wo": ("Wo1", "Wo2"),
     "bo": ("bo1", "bo2"), "g": ("g1", "g2", "g3"), "b": ("be1", "be2", "be3"),
     "w_up": "Wp", "b_up": "bp", "w_down": "W2", "b_down": "b2"},
]


def kernel(**inputs):
    import numpy as _np
    import concourse.bacc as _bacc
    from concourse import mybir as _mybir
    from concourse.bass_utils import run_bass_kernel_spmd as _run

    def layer(n, name):
        return _np.asarray(inputs[f"L{n}_xattn_{name}"])

    ls = range(len(_NAMES))
    columns, rows = [], []
    for n in ls:
        names = _NAMES[n]
        for g, b in zip(names["g"], names["b"]):
            columns += [layer(n, g), layer(n, b)]
        columns += list(layer(n, names["b_up"]).reshape(-1, 128))
        rows += [layer(n, names["bo"][0]), layer(n, names["bo"][1]), layer(n, names["b_down"])]
    arrays = {
        "x": _np.asarray(inputs["x"]),
        "ctx": _np.asarray(inputs["ctx_768"]),
        "wq": _np.stack([layer(n, m) for n in ls for m in _NAMES[n]["wq"]]),
        "wk_self": _np.stack([layer(n, _NAMES[n]["wk"][0]) for n in ls]),
        "wv_self": _np.stack([layer(n, _NAMES[n]["wv"][0]) for n in ls]),
        "wk_cross": _np.stack([layer(n, _NAMES[n]["wk"][1]) for n in ls]),
        "wv_cross": _np.stack([layer(n, _NAMES[n]["wv"][1]) for n in ls]),
        "wo": _np.stack([layer(n, m) for n in ls for m in _NAMES[n]["wo"]]),
        "w_up": _np.stack([layer(n, _NAMES[n]["w_up"]) for n in ls]),
        "w_down": _np.stack([layer(n, _NAMES[n]["w_down"]) for n in ls]),
        "columns": _np.stack(columns, axis=1),
        "rows": _np.stack(rows),
    }
    arrays = {f"in_{k}_dram": _np.ascontiguousarray(v) for k, v in arrays.items()}
    nc = _bacc.Bacc("TRN2", target_bir_lowering=False, num_devices=1)
    args = [nc.dram_tensor(k, v.shape, _mybir.dt.from_np(v.dtype), kind="ExternalInput").ap()
            for k, v in arrays.items()]
    out = nc.dram_tensor("out_0_dram", tuple(inputs["x"].shape), _mybir.dt.float32, kind="ExternalOutput").ap()
    transformer_kernel(nc, *args, out)
    r = _run(nc, [arrays], core_ids=[0])
    return r.results[0]["out_0_dram"]
```

```python
from contextlib import ExitStack

import concourse.bass as bass
from concourse import mybir

F32 = mybir.dt.float32
F32R = mybir.dt.float32r
I32 = mybir.dt.int32
ACT = mybir.ActivationFunctionType
ALU = mybir.AluOpType
AX = mybir.AxisListType

P = 128
EPS = 1e-5
RSQRT_MAGIC = 1597463007.0
NEWTON_STEPS = 3
LN_LINKS = 4 + 3 * NEWTON_STEPS + 3


def transformer_kernel(nc, x, ctx, wq, wk_self, wv_self, wk_cross, wv_cross, wo, w_up, w_down,
                       columns, rows, out):
    batches, seq, width = x.shape
    layers = w_up.shape[0]
    inner = wq.shape[2]
    ctx_width = ctx.shape[2]
    head_dim = 64
    pairs = inner // P
    tokens = batches * seq
    tiles = tokens // P
    halves = 2
    half = tokens // halves
    tiles_half = tiles // halves
    seq_tiles = seq // P
    units = batches * 2
    hidden = w_down.shape[1]
    hidden_tiles = hidden // P
    scale = float(head_dim) ** -0.5
    v_chunks = tiles * inner // 512
    n_cols = columns.shape[1] // layers
    G = {"self": 0, "cross": 2, "mlp": 4}
    B_UP = 6
    ROW = {"self": 0, "cross": 1, "mlp": 2}
    ATT = {"self": 0, "cross": 1}
    LN = {"self": 0, "cross": 1, "mlp": 2}
    assert width == P and seq == 256 and tokens == 1024 and units == 8 and pairs == 8

    with ExitStack() as stack:
        def sb(name, shape, dt=F32):
            return stack.enter_context(nc.sbuf_tensor(name, shape, dt))

        def sem(name):
            return stack.enter_context(nc.semaphore(name))

        def bank(name):
            return stack.enter_context(nc.psum_tensor(name, [P, 512], F32))

        ident = sb("ident", [P, P])
        cols = sb("cols", [P, layers * n_cols])
        rows_all = sb("rows_all", [P, layers * 3 * width])
        x_sb = sb("x_sb", [P, tiles, width])
        xn = sb("xn", [P, tiles, width])
        stats = sb("stats", [P, tiles, 6])
        mean_var = sb("mean_var", [P, tiles, 2])
        var_eps = sb("var_eps", [P, tiles])
        half_var = sb("half_var", [P, tiles])
        rstd = sb("rstd", [P, tiles])
        newton = sb("newton", [P, tiles])
        h_full = sb("h_full", [P, tokens])
        h_hi = sb("h_hi", [P, tokens], F32R)
        h_lo = sb("h_lo", [P, tokens], F32R)
        ctx_rows = sb("ctx_rows", [P, tiles, ctx_width])
        ctx_hi = sb("ctx_hi", [P, tokens], F32R)
        ctx_lo = sb("ctx_lo", [P, tokens], F32R)
        wq_raw = sb("wq_raw", [P, inner])
        wk_raw = sb("wk_raw", [P, inner])
        wv_raw = sb("wv_raw", [P, inner])
        wo_sb = sb("wo_sb", [P, pairs, width])
        w_down_sb = sb("w_down_sb", [P, hidden_tiles, width])
        wv_hi = sb("wv_hi", [P, inner], F32R)
        wv_lo = sb("wv_lo", [P, inner], F32R)
        wp_hi = sb("wp_hi", [P, 2, P], F32R)
        wp_lo = sb("wp_lo", [P, 2, P], F32R)
        w_up_raw = sb("w_up_raw", [P, 2 * hidden])
        w_up_hi = sb("w_up_hi", [P, 2 * hidden], F32R)
        w_up_lo = sb("w_up_lo", [P, 2 * hidden], F32R)
        qk_hi = [sb("q_hi", [P, tokens], F32R), sb("k_hi", [P, tokens], F32R)]
        qk_lo = [sb("q_lo", [P, tokens], F32R), sb("k_lo", [P, tokens], F32R)]
        v_sb = sb("v_sb", [P, tiles, inner])
        v_pair = sb("v_pair", [P, tiles, P])
        neg_max = sb("neg_max", [P, 4, seq_tiles])
        probs = sb("probs", [P, 4, seq_tiles, seq])
        row_sum = sb("row_sum", [P, 4, seq_tiles])
        inv_sum = sb("inv_sum", [P, 4, seq_tiles])
        probs_t = sb("probs_t", [P, 4, seq_tiles, seq])
        heads_t = sb("heads_t", [P, pairs, tokens])
        hidden_t = heads_t
        gate = sb("gate", [P, 2, half])
        credits = sb("credits", [P, 3])

        score_bank = [bank("score0"), bank("score1")]
        turn_bank = [bank("turn0"), bank("turn1")]
        pv_bank = [bank("pv0"), bank("pv1")]
        proj_bank = [bank("proj0"), bank("proj1")]

        x_loaded, ctx_loaded, cols_loaded, rows_loaded = (
            sem("x_loaded"), sem("ctx_loaded"), sem("cols_loaded"), sem("rows_loaded"))
        wv_loaded, wqk_loaded, wo_loaded = sem("wv_loaded"), sem("wqk_loaded"), sem("wo_loaded")
        w_up_loaded, w_down_loaded = sem("w_up_loaded"), sem("w_down_loaded")
        out_stored = sem("out_stored")
        v_pair_copied = [sem("v_pair_copied0"), sem("v_pair_copied1")]
        zeroed, ident_ready = sem("zeroed"), sem("ident_ready")
        ctx_turned, ctx_hi_ready, ctx_ready = sem("ctx_turned"), sem("ctx_hi_ready"), sem("ctx_ready")
        wv_split, pair_split, w_up_split = sem("wv_split"), sem("pair_split"), sem("w_up_split")
        v_made, qk_made = sem("v_made"), sem("qk_made")
        wo_used, w_down_used = sem("wo_used"), sem("w_down_used")
        pool_link = sem("pool_link")
        row_added = sem("row_added")
        ln_link, ln_turned, h_ready = sem("ln_link"), sem("ln_turned"), sem("h_ready")
        v_out_act, v_out_dve = sem("v_out_act"), sem("v_out_dve")
        qk_hi_out, qk_lo_out = sem("qk_hi_out"), sem("qk_lo_out")
        scored, maxed, exped, turned = sem("scored"), sem("maxed"), sem("exped"), sem("turned")
        turned_out_dve, turned_out_act = sem("turned_out_dve"), sem("turned_out_act")
        pv_made, inverted, normed = sem("pv_made"), sem("inverted"), sem("normed")
        heads_out_done = sem("heads_out_done")
        attended, residual_done = sem("attended"), sem("residual_done")
        up_made, gate_made, gate_done, hidden_done = (
            sem("up_made"), sem("gate_made"), sem("gate_done"), sem("hidden_done"))
        down_made = sem("down_made")

        def att_n(L, kind):
            return L * 2 + ATT[kind]

        def pair_n(L, kind, i):
            return L * (2 * pairs) + (ATT[kind] * pairs + i)

        def ln_n(L, kind, c):
            return L * (3 * halves) + (LN[kind] * halves + c)

        by_act, by_dve = (0, 2, 4, 6, 7), (1, 3, 5)

        def turned_out_by(n, u):
            if u in by_act:
                return turned_out_act, n * len(by_act) + (by_act.index(u) + 1)
            return turned_out_dve, n * len(by_dve) + (by_dve.index(u) + 1)

        v_by_dve = tuple(j for j in range(v_chunks // 2, v_chunks) if j % 2)
        v_by_act = tuple(j for j in range(v_chunks) if j not in v_by_dve)

        def v_out_by(n, j):
            if j in v_by_dve:
                return v_out_dve, n * len(v_by_dve) + (v_by_dve.index(j) + 1)
            return v_out_act, n * len(v_by_act) + (v_by_act.index(j) + 1)

        def half_cols(c):
            return slice(c * half, (c + 1) * half)

        def half_tiles(c):
            return range(c * tiles_half, (c + 1) * tiles_half)

        pool_held, pe_held, act_held, dve_held, sp_held = (
            sem("pool_held"), sem("pe_held"), sem("act_held"), sem("dve_held"), sem("sp_held"))

        def v_part(j):
            return v_sb[:, j // 2, (j % 2) * 512:(j % 2 + 1) * 512]

        block = stack.enter_context(nc.Block())

        @block.sync
        def _(sp):
            sp.dma_start(x_sb[:], x.rearrange("b (t p) d -> p (b t) d", p=P)).then_inc(x_loaded, 16)
            sp.dma_start(cols[:], columns).then_inc(cols_loaded, 16)
            sp.dma_start(ctx_rows[:], ctx.rearrange("b (t p) d -> p (b t) d", p=P)).then_inc(ctx_loaded, 16)

            def load_attention(L, kind):
                k_rows = P if kind == "self" else ctx_width
                wk, wv = (wk_self, wv_self) if kind == "self" else (wk_cross, wv_cross)
                n = att_n(L, kind)
                sp.wait_ge(wv_split, n + 1)
                sp.dma_start(wv_raw[0:k_rows, :], wv[bass.ds(L, 1)].rearrange("a p n -> (a p) n")
                             ).then_inc(wv_loaded, 16)
                sp.wait_ge(pair_split, n * pairs + 1)
                sp.dma_start(wq_raw[:], wq[bass.ds(n, 1)].rearrange("a p n -> (a p) n")
                             ).then_inc(wqk_loaded, 16)
                sp.dma_start(wk_raw[0:k_rows, :], wk[bass.ds(L, 1)].rearrange("a p n -> (a p) n")
                             ).then_inc(wqk_loaded, 16)
                sp.wait_ge(wo_used, n * halves + 1)
                sp.dma_start(wo_sb[:], wo[bass.ds(n, 1)].rearrange("a (i p) n -> p (a i) n", p=P)
                             ).then_inc(wo_loaded, 16)

            def copy_values(L, kind):
                n = att_n(L, kind)

                def copy_half(i, c, weighed):
                    sp.wait_ge(pv_made, weighed)
                    at = half_tiles(c)
                    at = slice(at[0], at[-1] + 1)
                    sp.dma_start(v_pair[:, at, :], v_sb[:, at, bass.ds(i * P, P)]).then_inc(v_pair_copied[c], 16)

                first = pair_n(L, kind, 0) * batches + 1
                sp.wait_ge(*v_out_by(n, v_chunks // 2 - 1))
                copy_half(0, 0, first)
                sp.wait_ge(*v_out_by(n, v_chunks - 2))
                sp.wait_ge(*v_out_by(n, v_chunks - 1))
                copy_half(0, 1, first)
                with sp.Fori(1, pairs) as i:
                    done = pair_n(L, kind, i) * batches + 1
                    copy_half(i, 0, done - batches // 2)
                    copy_half(i, 1, done)

            with sp.Fori(0, layers) as L:
                load_attention(L, "self")
                sp.wait_ge(w_up_split, L + 1)
                sp.dma_start(w_up_raw[:], w_up[bass.ds(L, 1)].rearrange("a p n -> (a p) n")
                             ).then_inc(w_up_loaded, 16)
                sp.wait_ge(w_down_used, L * halves + 1)
                sp.dma_start(w_down_sb[:], w_down[bass.ds(L, 1)].rearrange("a (f p) n -> p (a f) n", p=P)
                             ).then_inc(w_down_loaded, 16)
                copy_values(L, "self")
                load_attention(L, "cross")
                copy_values(L, "cross")

            sp.wait_ge(residual_done, layers * 3 * halves)
            sp.dma_start(out.rearrange("b (t p) d -> p (b t) d", p=P), x_sb[:]).then_inc(out_stored, 16)
            sp.wait_ge(out_stored, 16)

        @block.gpsimd
        def _(pool):
            pool.dma_start(rows_all[:], rows.rearrange("a n -> (a n)").partition_broadcast(P)
                           ).then_inc(rows_loaded, 16)
            pool.memset(ident[:], 0.0).then_inc(zeroed, 1)
            pool.wait_ge(zeroed, 1)
            pool.affine_select(out=ident[:], in_=ident[:], compare_op=ALU.not_equal, fill=1.0, base=0,
                               pattern=[[-1, P]], channel_multiplier=1).then_inc(ident_ready, 1)
            for k, credit in enumerate((wv_split, pair_split, w_up_split)):
                pool.memset(credits[:, k:k + 1], 0.0).then_inc(credit, 1)

            def split(hi, lo, raw, link, done):
                pool.tensor_copy(hi, raw).then_inc(pool_link, 1)
                pool.wait_ge(pool_link, link)
                return pool.tensor_tensor(lo, raw, hi.bitcast(F32), ALU.subtract).then_inc(done, 1)

            links_att = 1 + 2 * pairs
            links_layer = 2 * links_att + 1

            def split_pair(L, kind, i):
                k_rows = P if kind == "self" else ctx_width
                link = L * links_layer + (ATT[kind] * links_att + 1) + i * 2
                pool.wait_ge(qk_made, pair_n(L, kind, i) * 4 + 1)
                pool.sem_inc(pool_held, 1)
                at = bass.ds(i * P, P)
                pool.tensor_copy(wp_hi[:, 0, :], wq_raw[:, at]).then_inc(pool_link, 1)
                pool.tensor_copy(wp_hi[0:k_rows, 1, :], wk_raw[0:k_rows, at]).then_inc(pool_link, 1)
                pool.wait_ge(pool_link, link + 2)
                pool.sem_inc(pool_held, 1)
                pool.tensor_tensor(wp_lo[:, 0, :], wq_raw[:, at], wp_hi[:, 0, :].bitcast(F32), ALU.subtract)
                pool.tensor_tensor(wp_lo[0:k_rows, 1, :], wk_raw[0:k_rows, at],
                                   wp_hi[0:k_rows, 1, :].bitcast(F32), ALU.subtract).then_inc(pair_split, 1)

            def add_row(L, kind, c):
                pool.wait_ge(ln_link, ln_n(L, kind, c) * LN_LINKS + LN_LINKS - 2)
                pool.sem_inc(pool_held, 1)
                row = rows_all[:, bass.ds(L * (3 * width) + ROW[kind] * width, width)]
                for t in half_tiles(c):
                    last = pool.tensor_tensor(x_sb[:, t, :], x_sb[:, t, :], row, ALU.add)
                last.then_inc(row_added, 1)

            def attention(L, kind):
                k_rows = P if kind == "self" else ctx_width
                n = att_n(L, kind)
                pool.wait_ge(wv_loaded, (n + 1) * 16)
                pool.wait_ge(v_made, n * v_chunks + 1)
                pool.sem_inc(pool_held, 1)
                split(wv_hi[0:k_rows, :], wv_lo[0:k_rows, :], wv_raw[0:k_rows, :],
                      L * links_layer + ATT[kind] * links_att + 1, wv_split)
                pool.wait_ge(wqk_loaded, (n + 1) * 32)
                split_pair(L, kind, 0)
                for c in range(halves):
                    add_row(L, kind, c)
                with pool.Fori(1, pairs) as i:
                    split_pair(L, kind, i)

            pool.wait_ge(rows_loaded, 16)
            with pool.Fori(0, layers) as L:
                attention(L, "self")
                attention(L, "cross")
                pool.wait_ge(w_up_loaded, (L + 1) * 16)
                pool.wait_ge(w_down_used, L * halves + 1)
                pool.sem_inc(pool_held, 1)
                split(w_up_hi[:], w_up_lo[:], w_up_raw[:], (L + 1) * links_layer, w_up_split)
                for c in range(halves):
                    add_row(L, "mlp", c)

        @block.tensor
        def _(pe):
            def product(out_ap, st, mv):
                nc.tensor.matmul(out_ap, st[1], mv[0], start=True, stop=False)
                nc.tensor.matmul(out_ap, st[0], mv[1], start=False, stop=False)
                return nc.tensor.matmul(out_ap, st[0], mv[0], start=False, stop=True)

            def turn_norm(L, kind, c):
                pe.wait_ge(ln_link, ln_n(L, kind, c) * LN_LINKS + LN_LINKS - 2)
                for j, t in enumerate(half_tiles(c)):
                    last = nc.tensor.transpose(pv_bank[c][:, j * P:(j + 1) * P], xn[:, t, :], ident[:])
                last.then_inc(ln_turned, 1)

            def project_v(L, kind, chunks):
                k_rows, s_hi, s_lo = (P, h_hi, h_lo) if kind == "self" else (ctx_width, ctx_hi, ctx_lo)
                n = att_n(L, kind)
                for j in chunks:
                    t, part = j // 2, j % 2
                    if j >= 2:
                        pe.wait_ge(*v_out_by(n, j - 2))
                    at, to = slice(t * P, (t + 1) * P), slice(part * 512, (part + 1) * 512)
                    product(turn_bank[j % 2][:],
                            (s_hi[0:k_rows, at], s_lo[0:k_rows, at]),
                            (wv_hi[0:k_rows, to], wv_lo[0:k_rows, to])).then_inc(v_made, 1)

            def project_qk(kind, which, c, to_bank):
                k_rows, s_hi, s_lo = (P, h_hi, h_lo) if which == 0 or kind == "self" else (ctx_width, ctx_hi, ctx_lo)
                at = half_cols(c)
                product(proj_bank[to_bank][:],
                        (wp_hi[0:k_rows, which, :], wp_lo[0:k_rows, which, :]),
                        (s_hi[0:k_rows, at], s_lo[0:k_rows, at])).then_inc(qk_made, 1)

            def score(n, u, has_prev):
                b, hh = u // 2, u % 2
                if u == 0:
                    pe.wait_ge(qk_lo_out, n * 4 + 2)
                if u == units // 2:
                    pe.wait_ge(qk_lo_out, n * 4 + 4)
                if u >= 2 or has_prev:
                    pe.wait_ge(exped, n * units + (u - 1))
                head = slice(hh * head_dim, (hh + 1) * head_dim)
                keys = slice(b * seq, (b + 1) * seq)
                for s in range(seq_tiles):
                    qs = slice(b * seq + s * P, b * seq + (s + 1) * P)
                    m = product(score_bank[u % 2][:, s * seq:(s + 1) * seq],
                                (qk_hi[0][head, qs], qk_lo[0][head, qs]),
                                (qk_hi[1][head, keys], qk_lo[1][head, keys]))
                m.then_inc(scored, 1)

            def turn(n, u, has_prev=True):
                pe.wait_ge(normed, n * units + (u + 1))
                if u >= 2:
                    pe.wait_ge(*turned_out_by(n, u - 2))
                elif u == 0 and has_prev:
                    pe.wait_ge(*turned_out_by(n - 1, units - 2))
                for kt in range(seq_tiles):
                    for s in range(seq_tiles):
                        m = nc.tensor.transpose(
                            turn_bank[u % 2][:, kt * seq + s * P:kt * seq + (s + 1) * P],
                            probs[:, u % 4, s, kt * P:(kt + 1) * P], ident[:])
                m.then_inc(turned, 1)

            def weigh(n, b):
                if b % 2 == 0:
                    pe.wait_ge(v_pair_copied[b // 2], (n + 1) * 16)
                if b >= 2:
                    pe.wait_ge(heads_out_done, n * batches + (b - 1))
                pe.wait_ge(*turned_out_by(n, 2 * b))
                pe.wait_ge(*turned_out_by(n, 2 * b + 1))
                for kt in range(seq_tiles):
                    for hh in range(2):
                        head = slice(hh * head_dim, (hh + 1) * head_dim)
                        m = nc.tensor.matmul(pv_bank[b % 2][head, 0:seq],
                                             v_pair[:, b * seq_tiles + kt, head],
                                             probs_t[:, (2 * b + hh) % 4, kt, :],
                                             start=(kt == 0), stop=(kt == seq_tiles - 1))
                m.then_inc(pv_made, 1)

            def pair_body(L, kind, i, has_prev, has_next):
                n = pair_n(L, kind, i)
                score(n, 0, has_prev)
                if has_prev:
                    project_qk(kind, 0, 1, 0)
                    turn(n - 1, 5)
                else:
                    if kind == "self":
                        pe.wait_ge(h_ready, ln_n(L, kind, 1) + 1)
                    project_v(L, kind, range(v_chunks // 2, v_chunks // 2 + 4))
                    pe.wait_ge(h_ready, ln_n(L, kind, 1) + 1)
                    project_qk(kind, 0, 1, 0)
                score(n, 1, has_prev)
                project_qk(kind, 1, 1, 1)
                if has_prev:
                    turn(n - 1, 6)
                else:
                    project_v(L, kind, range(v_chunks // 2 + 4, v_chunks - 2))
                score(n, 2, has_prev)
                if has_prev:
                    turn(n - 1, 7)
                    weigh(n - 1, 2)
                else:
                    project_v(L, kind, range(v_chunks - 2, v_chunks))
                score(n, 3, has_prev)
                if not has_prev:
                    pe.wait_ge(*v_out_by(att_n(L, kind), v_chunks - 2))
                    pe.wait_ge(*v_out_by(att_n(L, kind), v_chunks - 1))
                turn(n, 0, has_prev)
                if has_prev:
                    weigh(n - 1, 3)
                score(n, 4, has_prev)
                if has_next:
                    pe.wait_ge(pair_split, n + 3)
                    project_qk(kind, 0, 0, 0)
                turn(n, 1)
                score(n, 5, has_prev)
                if has_next:
                    project_qk(kind, 1, 0, 1)
                turn(n, 2)
                score(n, 6, has_prev)
                turn(n, 3)
                weigh(n, 0)
                score(n, 7, has_prev)
                turn(n, 4)
                weigh(n, 1)

            def last_units(L, kind, then):
                n = pair_n(L, kind, pairs - 1)
                turn(n, 5)
                project_out(L, kind, 0, (0, 1))
                turn(n, 6)
                weigh(n, 2)
                turn(n, 7)
                project_out(L, kind, 0, (2, 3))
                weigh(n, 3)
                project_out(L, kind, 1, (4, 5, 6))
                turn_norm(L, then, 0)
                project_out(L, kind, 1, (7,))

            def project_out(L, kind, c, some_tiles):
                if some_tiles[0] % tiles_half == 0:
                    pe.wait_ge(wo_loaded, (att_n(L, kind) + 1) * 16)
                done = some_tiles[-1] // seq_tiles + 1
                pe.wait_ge(heads_out_done, (pair_n(L, kind, pairs - 1)) * batches + done)
                for t in some_tiles:
                    j = t % tiles_half
                    for i in range(pairs):
                        m = nc.tensor.matmul(score_bank[c][:, j * P:(j + 1) * P],
                                             heads_t[:, i, t * P:(t + 1) * P], wo_sb[:, i, :],
                                             start=(i == 0), stop=(i == pairs - 1))
                if some_tiles[-1] % tiles_half == tiles_half - 1:
                    m.then_inc(wo_used, 1)

            def attention(L, kind):
                n = att_n(L, kind)
                if kind == "self":
                    turn_norm(L, kind, 0)
                    pe.wait_ge(h_ready, ln_n(L, kind, 0) + 1)
                pe.wait_ge(wv_split, n + 2)
                project_v(L, kind, range(0, v_chunks // 2))
                pe.wait_ge(pair_split, n * pairs + 2)
                pe.wait_ge(h_ready, ln_n(L, kind, 0) + 1)
                project_qk(kind, 0, 0, 0)
                project_qk(kind, 1, 0, 1)
                turn_norm(L, kind, 1)
                pair_body(L, kind, 0, False, True)
                pe.sem_inc(pe_held, 1)
                with pe.Fori(1, pairs - 1) as i:
                    pair_body(L, kind, i, True, True)
                pair_body(L, kind, pairs - 1, True, False)
                last_units(L, kind, "cross" if kind == "self" else "mlp")

            def mlp(L):
                n = L * (halves * hidden_tiles)
                pe.wait_ge(w_up_split, L + 2)
                for c in range(halves):
                    if c == 1:
                        turn_norm(L, "mlp", 1)
                    pe.wait_ge(h_ready, ln_n(L, "mlp", c) + 1)
                    for f in range(hidden_tiles):
                        j = c * hidden_tiles + f
                        for which, to in ((1, score_bank), (0, turn_bank)):
                            if which == 1 and c == 0 and f < 2:
                                pe.wait_ge(residual_done, L * (3 * halves) + halves + f + 1)
                            if j >= 2:
                                pe.wait_ge((hidden_done, gate_done)[which], n + j - 1)
                            at = slice(which * hidden + f * P, which * hidden + (f + 1) * P)
                            product(to[j % 2][:], (w_up_hi[:, at], w_up_lo[:, at]),
                                    (h_hi[:, half_cols(c)], h_lo[:, half_cols(c)])
                                    ).then_inc((up_made, gate_made)[which], 1)
                pe.wait_ge(w_down_loaded, (L + 1) * 16)
                for c in range(halves):
                    pe.wait_ge(hidden_done, n + (c + 1) * hidden_tiles)
                    for t in half_tiles(c):
                        j = t % tiles_half
                        for f in range(hidden_tiles):
                            m = nc.tensor.matmul(proj_bank[c][:, j * P:(j + 1) * P],
                                                 hidden_t[:, f, t * P:(t + 1) * P], w_down_sb[:, f, :],
                                                 start=(f == 0), stop=(f == hidden_tiles - 1))
                    m.then_inc(w_down_used, 1)

            pe.wait_ge(ident_ready, 1)
            pe.wait_ge(ctx_loaded, 16)
            for c in range(halves):
                for j, t in enumerate(half_tiles(c)):
                    m = nc.tensor.transpose(turn_bank[c][0:ctx_width, j * P:(j + 1) * P],
                                            ctx_rows[:, t, :], ident[:])
                m.then_inc(ctx_turned, 1)
            for credit in (v_made, qk_made, wo_used, w_down_used, pv_made):
                nc.tensor.transpose(pv_bank[0][0:ctx_width, 0:P], ctx_rows[:, 0, :], ident[:]).then_inc(credit, 1)
            pe.wait_ge(ctx_ready, halves)
            with pe.Fori(0, layers) as L:
                attention(L, "self")
                attention(L, "cross")
                mlp(L)

        @block.scalar
        def _(act):
            def v_out(L, kind, chunks):
                n = att_n(L, kind)
                for j in chunks:
                    if j not in v_by_act:
                        continue
                    act.wait_ge(v_made, n * v_chunks + j + 2)
                    nc.scalar.activation(v_part(j), turn_bank[j % 2][:], ACT.Copy).then_inc(v_out_act, 1)

            def qk_high(n, j, which, c, from_bank):
                act.wait_ge(qk_made, n * 4 + j + 2)
                nc.scalar.activation(qk_hi[which][:, half_cols(c)], proj_bank[from_bank][:], ACT.Copy,
                                     scale=(scale, 1.0)[which]).then_inc(qk_hi_out, 1)

            def exponentials(n, u):
                act.wait_ge(maxed, n * units + u + 1)
                for s in range(seq_tiles):
                    m = nc.scalar.activation(probs[:, u % 4, s, :], score_bank[u % 2][:, s * seq:(s + 1) * seq],
                                             ACT.Exp, bias=neg_max[:, u % 4, s:s + 1],
                                             accum_out=row_sum[:, u % 4, s:s + 1])
                m.then_inc(exped, 1)

            def turned_out(n, u):
                act.wait_ge(turned, n * units + (u + 1))
                nc.scalar.activation(probs_t[:, u % 4, :, :].rearrange("p a b -> p (a b)"),
                                     turn_bank[u % 2][:], ACT.Copy).then_inc(turned_out_act, 1)

            def heads_t_out(n, i, b):
                act.wait_ge(pv_made, n * batches + (b + 2))
                act.sem_inc(act_held, 1)
                nc.scalar.activation(heads_t[:, bass.ds(i, 1), b * seq:(b + 1) * seq].rearrange("p a b -> p (a b)"),
                                     pv_bank[b % 2][:, 0:seq], ACT.Copy).then_inc(heads_out_done, 1)

            def pair_body(L, kind, i, has_prev, has_next):
                n = pair_n(L, kind, i)
                exponentials(n, 0)
                if has_prev:
                    qk_high(n, 2, 0, 1, 0)
                    turned_out(n - 1, 6)
                else:
                    v_out(L, kind, range(v_chunks // 2, v_chunks // 2 + 4))
                    qk_high(n, 2, 0, 1, 0)
                exponentials(n, 1)
                qk_high(n, 3, 1, 1, 1)
                if has_prev:
                    turned_out(n - 1, 7)
                else:
                    v_out(L, kind, range(v_chunks // 2 + 4, v_chunks - 2))
                exponentials(n, 2)
                if has_prev:
                    heads_t_out(n - 1, i - 1, 2)
                else:
                    v_out(L, kind, range(v_chunks - 2, v_chunks))
                turned_out(n, 0)
                exponentials(n, 3)
                if has_prev:
                    heads_t_out(n - 1, i - 1, 3)
                exponentials(n, 4)
                if has_next:
                    qk_high(n, 4, 0, 0, 0)
                turned_out(n, 2)
                exponentials(n, 5)
                if has_next:
                    qk_high(n, 5, 1, 0, 1)
                exponentials(n, 6)
                heads_t_out(n, i, 0)
                turned_out(n, 4)
                exponentials(n, 7)
                heads_t_out(n, i, 1)

            def attention(L, kind):
                n = pair_n(L, kind, 0)
                v_out(L, kind, range(0, v_chunks // 2))
                qk_high(n, 0, 0, 0, 0)
                qk_high(n, 1, 1, 0, 1)
                pair_body(L, kind, 0, False, True)
                with act.Fori(1, pairs - 1) as i:
                    pair_body(L, kind, i, True, True)
                pair_body(L, kind, pairs - 1, True, False)
                last = pair_n(L, kind, pairs - 1)
                turned_out(last, 6)
                heads_t_out(last, pairs - 1, 2)
                turned_out(last, 7)
                heads_t_out(last, pairs - 1, 3)

            act.wait_ge(cols_loaded, 16)
            with act.Fori(0, layers) as L:
                attention(L, "self")
                attention(L, "cross")
                n = L * (halves * hidden_tiles)
                for j in range(halves * hidden_tiles):
                    f = j % hidden_tiles
                    act.wait_ge(gate_made, n + j + 1)
                    if j >= 2:
                        act.wait_ge(hidden_done, n + j - 1)
                    act.sem_inc(act_held, 1)
                    nc.scalar.activation(gate[:, j % 2, :], score_bank[j % 2][:], ACT.Gelu,
                                         bias=cols[:, bass.ds(L * n_cols + (B_UP + hidden_tiles + f), 1)]
                                         ).then_inc(gate_done, 1)

        @block.vector
        def _(dve):
            def norm_rows(L, kind, c):
                base = ln_n(L, kind, c) * LN_LINKS
                ts = half_tiles(c)
                h = slice(ts[0], ts[-1] + 1)
                for t in ts:
                    m = nc.vector.bn_stats(stats[:, t, :], x_sb[:, t, :])
                m.then_inc(ln_link, 1)
                dve.wait_ge(ln_link, base + 1)
                dve.sem_inc(dve_held, 1)
                for t in ts:
                    m = nc.vector.bn_aggr(mean_var[:, t, :], stats[:, t, :])
                m.then_inc(ln_link, 1)
                dve.wait_ge(ln_link, base + 2)
                nc.vector.tensor_scalar(half_var[:, h], mean_var[:, h, 1], -0.5, -0.5 * EPS, ALU.mult, ALU.add)
                nc.vector.tensor_scalar(var_eps[:, h], mean_var[:, h, 1], EPS, None, ALU.add).then_inc(ln_link, 1)
                dve.wait_ge(ln_link, base + 3)
                nc.vector.tensor_scalar(rstd[:, h].bitcast(I32), var_eps[:, h].bitcast(I32), -0.5, RSQRT_MAGIC,
                                        ALU.mult, ALU.add).then_inc(ln_link, 1)
                for k in range(NEWTON_STEPS):
                    dve.wait_ge(ln_link, base + 4 + 3 * k)
                    nc.vector.tensor_tensor(newton[:, h], rstd[:, h], rstd[:, h], ALU.mult).then_inc(ln_link, 1)
                    dve.wait_ge(ln_link, base + 5 + 3 * k)
                    nc.vector.tensor_tensor(newton[:, h], newton[:, h], half_var[:, h], ALU.mult).then_inc(ln_link, 1)
                    dve.wait_ge(ln_link, base + 6 + 3 * k)
                    nc.vector.scalar_tensor_tensor(out=rstd[:, h], in0=newton[:, h], scalar=1.5, in1=rstd[:, h],
                                                   op0=ALU.add, op1=ALU.mult).then_inc(ln_link, 1)
                dve.wait_ge(ln_link, base + LN_LINKS - 3)
                for t in ts:
                    m = nc.vector.tensor_scalar(xn[:, t, :], x_sb[:, t, :], mean_var[:, t, 0:1], rstd[:, t:t + 1],
                                                ALU.subtract, ALU.mult)
                m.then_inc(ln_link, 1)

            def norm_parts(L, kind, c):
                n = ln_n(L, kind, c)
                at = half_cols(c)
                dve.wait_ge(ln_turned, n + 1)
                nc.vector.tensor_scalar(h_full[:, at], pv_bank[c][:],
                                        cols[:, bass.ds(L * n_cols + G[kind], 1)],
                                        cols[:, bass.ds(L * n_cols + G[kind] + 1, 1)],
                                        ALU.mult, ALU.add).then_inc(ln_link, 1)
                dve.wait_ge(ln_link, n * LN_LINKS + LN_LINKS - 1)
                nc.vector.tensor_copy(h_hi[:, at], h_full[:, at]).then_inc(ln_link, 1)
                dve.wait_ge(ln_link, n * LN_LINKS + LN_LINKS)
                nc.vector.tensor_tensor(h_lo[:, at], h_full[:, at], h_hi[:, at].bitcast(F32),
                                        ALU.subtract).then_inc(h_ready, 1)

            def residual(L, stage, c, from_bank):
                n = L * (3 * halves) + LN[stage] * halves + c
                dve.wait_ge(row_added, n + 1)
                at = half_tiles(c)
                rows_c = x_sb[:, at[0]:at[-1] + 1, :].rearrange("p t d -> p (t d)")
                nc.vector.tensor_tensor(rows_c, from_bank[:], rows_c, ALU.add).then_inc(residual_done, 1)
                return n + 1

            def v_out(L, kind, chunks):
                n = att_n(L, kind)
                for j in chunks:
                    if j not in v_by_dve:
                        continue
                    dve.wait_ge(v_made, n * v_chunks + j + 2)
                    nc.vector.tensor_copy(v_part(j), turn_bank[j % 2][:]).then_inc(v_out_dve, 1)

            def qk_low(n, j, which, c, from_bank):
                dve.wait_ge(qk_hi_out, n * 4 + j + 1)
                nc.vector.scalar_tensor_tensor(out=qk_lo[which][:, half_cols(c)], in0=proj_bank[from_bank][:],
                                               scalar=(scale, 1.0)[which],
                                               in1=qk_hi[which][:, half_cols(c)].bitcast(F32),
                                               op0=ALU.mult, op1=ALU.subtract).then_inc(qk_lo_out, 1)

            def maxima(n, u):
                dve.wait_ge(scored, n * units + u + 1)
                nc.vector.tensor_reduce(neg_max[:, u % 4, :],
                                        score_bank[u % 2][:].rearrange("p (s k) -> p s k", k=seq),
                                        AX.X, ALU.max, negate=True).then_inc(maxed, 1)

            def turned_out(n, u):
                dve.wait_ge(turned, n * units + (u + 1))
                nc.vector.tensor_copy(probs_t[:, u % 4, :, :].rearrange("p a b -> p (a b)"),
                                      turn_bank[u % 2][:]).then_inc(turned_out_dve, 1)

            def normalise(n, u):
                dve.wait_ge(exped, n * units + (u + 1))
                nc.vector.reciprocal(inv_sum[:, u % 4, :], row_sum[:, u % 4, :]).then_inc(inverted, 1)
                dve.wait_ge(inverted, n * units + (u + 1))
                for s in range(seq_tiles):
                    m = nc.vector.tensor_scalar(probs[:, u % 4, s, :], probs[:, u % 4, s, :],
                                                inv_sum[:, u % 4, s:s + 1], None, ALU.mult)
                m.then_inc(normed, 1)

            def pair_body(L, kind, i, has_prev, has_next):
                n = pair_n(L, kind, i)
                maxima(n, 0)
                if has_prev:
                    normalise(n - 1, 7)
                    turned_out(n - 1, 5)
                else:
                    v_out(L, kind, range(v_chunks // 2, v_chunks // 2 + 4))
                maxima(n, 1)
                normalise(n, 0)
                qk_low(n, 2, 0, 1, 0)
                if not has_prev:
                    v_out(L, kind, range(v_chunks // 2 + 4, v_chunks - 2))
                maxima(n, 2)
                normalise(n, 1)
                qk_low(n, 3, 1, 1, 1)
                if not has_prev:
                    v_out(L, kind, range(v_chunks - 2, v_chunks))
                maxima(n, 3)
                normalise(n, 2)
                maxima(n, 4)
                normalise(n, 3)
                turned_out(n, 1)
                maxima(n, 5)
                if has_next:
                    qk_low(n, 4, 0, 0, 0)
                normalise(n, 4)
                maxima(n, 6)
                turned_out(n, 3)
                if has_next:
                    qk_low(n, 5, 1, 0, 1)
                normalise(n, 5)
                maxima(n, 7)
                normalise(n, 6)

            def attention(L, kind):
                n = pair_n(L, kind, 0)
                norm_parts(L, kind, 0)
                if kind == "self":
                    norm_rows(L, kind, 1)
                else:
                    sum_then_norm(L, "self", "cross", 1)
                qk_low(n, 0, 0, 0, 0)
                qk_low(n, 1, 1, 0, 1)
                norm_parts(L, kind, 1)
                pair_body(L, kind, 0, False, True)
                with dve.Fori(1, pairs - 1) as i:
                    pair_body(L, kind, i, True, True)
                pair_body(L, kind, pairs - 1, True, False)
                last = pair_n(L, kind, pairs - 1)
                normalise(last, 7)
                turned_out(last, 5)

            def sum_then_norm(L, stage, then, c):
                dve.wait_ge(wo_used, att_n(L, stage) * halves + c + 2)
                done = residual(L, stage, c, score_bank[c])
                dve.wait_ge(residual_done, done)
                norm_rows(L, then, c)

            dve.wait_ge(cols_loaded, 16)
            for c in range(halves):
                dve.wait_ge(ctx_turned, c + 1)
                at = half_cols(c)
                nc.vector.tensor_copy(ctx_hi[0:ctx_width, at], turn_bank[c][0:ctx_width, :]).then_inc(ctx_hi_ready, 1)
                dve.wait_ge(ctx_hi_ready, c + 1)
                nc.vector.tensor_tensor(ctx_lo[0:ctx_width, at], turn_bank[c][0:ctx_width, :],
                                        ctx_hi[0:ctx_width, at].bitcast(F32), ALU.subtract).then_inc(ctx_ready, 1)
            dve.wait_ge(x_loaded, 16)
            with dve.Fori(0, layers) as L:
                norm_rows(L, "self", 0)
                attention(L, "self")
                sum_then_norm(L, "self", "cross", 0)
                attention(L, "cross")
                sum_then_norm(L, "cross", "mlp", 0)
                norm_parts(L, "mlp", 0)
                sum_then_norm(L, "cross", "mlp", 1)
                n = L * (halves * hidden_tiles)
                for c in range(halves):
                    if c == 1:
                        norm_parts(L, "mlp", 1)
                    for f in range(hidden_tiles):
                        j = c * hidden_tiles + f
                        dve.wait_ge(up_made, n + j + 1)
                        dve.wait_ge(gate_done, n + j + 1)
                        nc.vector.scalar_tensor_tensor(out=hidden_t[:, f, half_cols(c)], in0=turn_bank[j % 2][:],
                                                       scalar=cols[:, bass.ds(L * n_cols + (B_UP + f), 1)],
                                                       in1=gate[:, j % 2, :],
                                                       op0=ALU.add, op1=ALU.mult).then_inc(hidden_done, 1)
                for c in range(halves):
                    dve.wait_ge(w_down_used, L * halves + c + 2)
                    done = residual(L, "mlp", c, proj_bank[c])
                dve.wait_ge(residual_done, done)


_NAMES = [
    {"wq": ("wq1", "wq2"), "wk": ("wk1", "wk2"), "wv": ("wv1", "wv2"), "wo": ("wo1", "wo2"),
     "bo": ("bo1", "bo2"), "g": ("g1", "g2", "g3"), "b": ("b1", "b2", "b3"),
     "w_up": "w_ff1", "b_up": "b_ff1", "w_down": "w_ff2", "b_down": "b_ff2"},
    {"wq": ("Wq1", "Wq2"), "wk": ("Wk1", "Wk2"), "wv": ("Wv1", "Wv2"), "wo": ("Wo1", "Wo2"),
     "bo": ("bo1", "bo2"), "g": ("g1", "g2", "g3"), "b": ("be1", "be2", "be3"),
     "w_up": "Wp", "b_up": "bp", "w_down": "W2", "b_down": "b2"},
]


def kernel(**inputs):
    import numpy as _np
    import concourse.bacc as _bacc
    from concourse import mybir as _mybir
    from concourse.bass_utils import run_bass_kernel_spmd as _run

    def layer(n, name):
        return _np.asarray(inputs[f"L{n}_xattn_{name}"])

    ls = range(len(_NAMES))
    columns, rows = [], []
    for n in ls:
        names = _NAMES[n]
        for g, b in zip(names["g"], names["b"]):
            columns += [layer(n, g), layer(n, b)]
        columns += list(layer(n, names["b_up"]).reshape(-1, 128))
        rows += [layer(n, names["bo"][0]), layer(n, names["bo"][1]), layer(n, names["b_down"])]
    arrays = {
        "x": _np.asarray(inputs["x"]),
        "ctx": _np.asarray(inputs["ctx_768"]),
        "wq": _np.stack([layer(n, m) for n in ls for m in _NAMES[n]["wq"]]),
        "wk_self": _np.stack([layer(n, _NAMES[n]["wk"][0]) for n in ls]),
        "wv_self": _np.stack([layer(n, _NAMES[n]["wv"][0]) for n in ls]),
        "wk_cross": _np.stack([layer(n, _NAMES[n]["wk"][1]) for n in ls]),
        "wv_cross": _np.stack([layer(n, _NAMES[n]["wv"][1]) for n in ls]),
        "wo": _np.stack([layer(n, m) for n in ls for m in _NAMES[n]["wo"]]),
        "w_up": _np.stack([layer(n, _NAMES[n]["w_up"]) for n in ls]),
        "w_down": _np.stack([layer(n, _NAMES[n]["w_down"]) for n in ls]),
        "columns": _np.stack(columns, axis=1),
        "rows": _np.stack(rows),
    }
    arrays = {f"in_{k}_dram": _np.ascontiguousarray(v) for k, v in arrays.items()}
    nc = _bacc.Bacc("TRN2", target_bir_lowering=False, num_devices=1)
    args = [nc.dram_tensor(k, v.shape, _mybir.dt.from_np(v.dtype), kind="ExternalInput").ap()
            for k, v in arrays.items()]
    out = nc.dram_tensor("out_0_dram", tuple(inputs["x"].shape), _mybir.dt.float32, kind="ExternalOutput").ap()
    transformer_kernel(nc, *args, out)
    r = _run(nc, [arrays], core_ids=[0])
    return r.results[0]["out_0_dram"]
```

```python
from contextlib import ExitStack

import concourse.bass as bass
from concourse import mybir

F32 = mybir.dt.float32
F32R = mybir.dt.float32r
I32 = mybir.dt.int32
ACT = mybir.ActivationFunctionType
ALU = mybir.AluOpType
AX = mybir.AxisListType

P = 128
EPS = 1e-5
RSQRT_MAGIC = 1597463007.0
NEWTON_STEPS = 3
LN_LINKS = 5 + 2 * NEWTON_STEPS + 1


def transformer_kernel(nc, x, ctx, wq, wk_self, wv_self, wk_cross, wv_cross, wo, w_up, w_down,
                       columns, rows, out):
    batches, seq, width = x.shape
    layers = w_up.shape[0]
    inner = wq.shape[2]
    ctx_width = ctx.shape[2]
    head_dim = 64
    pairs = inner // P
    tokens = batches * seq
    tiles = tokens // P
    halves = 2
    half = tokens // halves
    tiles_half = tiles // halves
    seq_tiles = seq // P
    units = batches * 2
    hidden = w_down.shape[1]
    hidden_tiles = hidden // P
    scale = float(head_dim) ** -0.5
    v_chunks = tiles * inner // 512
    n_cols = columns.shape[1] // layers
    G = {"self": 0, "cross": 2, "mlp": 4}
    B_UP = 6
    ROW = {"self": 0, "cross": 1, "mlp": 2}
    ATT = {"self": 0, "cross": 1}
    LN = {"self": 0, "cross": 1, "mlp": 2}
    assert width == P and seq == 256 and tokens == 1024 and units == 8 and pairs == 8

    with ExitStack() as stack:
        def sb(name, shape, dt=F32):
            return stack.enter_context(nc.sbuf_tensor(name, shape, dt))

        def sem(name):
            return stack.enter_context(nc.semaphore(name))

        def bank(name):
            return stack.enter_context(nc.psum_tensor(name, [P, 512], F32))

        ident = sb("ident", [P, P])
        cols = sb("cols", [P, layers * n_cols])
        rows_all = sb("rows_all", [P, layers * 3 * width])
        x_sb = sb("x_sb", [P, tiles, width])
        xn = sb("xn", [P, tiles, width])
        stats = sb("stats", [P, tiles, 6])
        mean_var = sb("mean_var", [P, tiles, 2])
        var_eps = sb("var_eps", [P, tiles])
        half_var = sb("half_var", [P, tiles])
        rstd = sb("rstd", [P, tiles])
        newton = sb("newton", [P, tiles])
        half_root = sb("half_root", [P, tiles])
        h_full = sb("h_full", [P, tokens])
        h_hi = sb("h_hi", [P, tokens], F32R)
        h_lo = sb("h_lo", [P, tokens], F32R)
        ctx_rows = sb("ctx_rows", [P, tiles, ctx_width])
        ctx_hi = sb("ctx_hi", [P, tokens], F32R)
        ctx_lo = sb("ctx_lo", [P, tokens], F32R)
        wq_raw = sb("wq_raw", [P, inner])
        wk_raw = sb("wk_raw", [P, inner])
        wv_raw = sb("wv_raw", [P, inner])
        wo_sb = sb("wo_sb", [P, pairs, width])
        w_down_sb = sb("w_down_sb", [P, hidden_tiles, width])
        wv_hi = sb("wv_hi", [P, inner], F32R)
        wv_lo = sb("wv_lo", [P, inner], F32R)
        wp_hi = sb("wp_hi", [P, 2, P], F32R)
        wp_lo = sb("wp_lo", [P, 2, P], F32R)
        w_up_raw = sb("w_up_raw", [P, 2 * hidden])
        w_up_hi = sb("w_up_hi", [P, 2 * hidden], F32R)
        w_up_lo = sb("w_up_lo", [P, 2 * hidden], F32R)
        qk_hi = [sb("q_hi", [P, tokens], F32R), sb("k_hi", [P, tokens], F32R)]
        qk_lo = [sb("q_lo", [P, tokens], F32R), sb("k_lo", [P, tokens], F32R)]
        v_sb = sb("v_sb", [P, tiles, inner])
        v_pair = sb("v_pair", [P, tiles, P])
        neg_max = sb("neg_max", [P, 4, seq_tiles])
        probs = sb("probs", [P, 4, seq_tiles, seq])
        row_sum = sb("row_sum", [P, 4, seq_tiles])
        inv_sum = sb("inv_sum", [P, 4, seq_tiles])
        probs_t = sb("probs_t", [P, 4, seq_tiles, seq])
        heads_t = sb("heads_t", [P, pairs, tokens])
        hidden_t = heads_t
        gate = probs_t[:].rearrange("p u k q -> p u (k q)")
        credits = sb("credits", [P, 3])
        table_scratch = sb("table_scratch", [P, 1])

        score_bank = [bank("score0"), bank("score1")]
        turn_bank = [bank("turn0"), bank("turn1")]
        pv_bank = [bank("pv0"), bank("pv1")]
        proj_bank = [bank("proj0"), bank("proj1")]
        up_bank = turn_bank + proj_bank

        x_loaded = [sem("x_loaded0"), sem("x_loaded1")]
        ctx_loaded, cols_loaded, rows_loaded = (
            sem("ctx_loaded"), sem("cols_loaded"), sem("rows_loaded"))
        wv_loaded, wqk_loaded, wo_loaded = sem("wv_loaded"), sem("wqk_loaded"), sem("wo_loaded")
        w_up_loaded, w_down_loaded = sem("w_up_loaded"), sem("w_down_loaded")
        out_stored = [sem("out_stored0"), sem("out_stored1")]
        v_pair_copied = [sem("v_pair_copied0"), sem("v_pair_copied1")]
        zeroed, ident_ready = sem("zeroed"), sem("ident_ready")
        ctx_turned, ctx_hi_ready, ctx_ready = sem("ctx_turned"), sem("ctx_hi_ready"), sem("ctx_ready")
        wv_split, pair_split, w_up_split = sem("wv_split"), sem("pair_split"), sem("w_up_split")
        v_made, qk_made = sem("v_made"), sem("qk_made")
        wo_used, w_down_used = sem("wo_used"), sem("w_down_used")
        pool_link = sem("pool_link")
        row_added = sem("row_added")
        ln_link, ln_turned, h_full_ready, h_ready = (
            sem("ln_link"), sem("ln_turned"), sem("h_full_ready"), sem("h_ready"))
        v_out_act, v_out_dve = sem("v_out_act"), sem("v_out_dve")
        qk_hi_out, qk_lo_out = sem("qk_hi_out"), sem("qk_lo_out")
        scored, maxed, exped, turned = sem("scored"), sem("maxed"), sem("exped"), sem("turned")
        turned_out_dve, turned_out_act = sem("turned_out_dve"), sem("turned_out_act")
        pv_made, inverted = sem("pv_made"), sem("inverted")
        normed_pool, normed_dve = sem("normed_pool"), sem("normed_dve")
        heads_out_done = sem("heads_out_done")
        residual_done = sem("residual_done")
        up_made, gate_made, gate_done, up_out = (
            sem("up_made"), sem("gate_made"), sem("gate_done"), sem("up_out"))
        hidden_done_pool, hidden_done_dve = sem("hidden_done_pool"), sem("hidden_done_dve")

        def att_n(L, kind):
            return L * 2 + ATT[kind]

        def pair_n(L, kind, i):
            return L * (2 * pairs) + (ATT[kind] * pairs + i)

        def ln_n(L, kind, c):
            return L * (3 * halves) + (LN[kind] * halves + c)

        by_act, by_dve = (0, 2, 4, 6, 7), (1, 3, 5)
        norm_by_pool = (1, 3, 5)
        norm_by_dve = tuple(u for u in range(units) if u not in norm_by_pool)

        def normed_by(n, u):
            if u in norm_by_pool:
                return normed_pool, n * len(norm_by_pool) + (norm_by_pool.index(u) + 1)
            return normed_dve, n * len(norm_by_dve) + (norm_by_dve.index(u) + 1)

        def turned_out_by(n, u):
            if u in by_act:
                return turned_out_act, n * len(by_act) + (by_act.index(u) + 1)
            return turned_out_dve, n * len(by_dve) + (by_dve.index(u) + 1)

        v_by_dve = tuple(j for j in range(v_chunks // 2, v_chunks) if j % 2 == 0)
        v_by_act = tuple(j for j in range(v_chunks) if j not in v_by_dve)

        def v_out_by(n, j):
            if j in v_by_dve:
                return v_out_dve, n * len(v_by_dve) + (v_by_dve.index(j) + 1)
            return v_out_act, n * len(v_by_act) + (v_by_act.index(j) + 1)

        gated_by_pool = 2
        gated_by_dve = hidden_tiles - gated_by_pool

        def gated_by(L, j):
            c, f = j // hidden_tiles, j % hidden_tiles
            if f < gated_by_pool:
                return hidden_done_pool, L * (halves * gated_by_pool) + (c * gated_by_pool + f + 1)
            return hidden_done_dve, L * (halves * gated_by_dve) + (c * gated_by_dve + f - gated_by_pool + 1)

        def half_cols(c):
            return slice(c * half, (c + 1) * half)

        def half_tiles(c):
            return range(c * tiles_half, (c + 1) * tiles_half)

        pool_held, pe_held, act_held, dve_held = (
            sem("pool_held"), sem("pe_held"), sem("act_held"), sem("dve_held"))

        def v_chunk(j):
            c, part, t = j // (2 * tiles_half), j // tiles_half % 2, j % tiles_half
            return c * tiles_half + t, slice(part * 512, (part + 1) * 512)

        def v_bank(j):
            if j < v_chunks // 2:
                return (turn_bank + [pv_bank[1]])[j % 3]
            return turn_bank[j % 2]

        def v_part(j):
            t, at = v_chunk(j)
            return v_sb[:, t, at]

        block = stack.enter_context(nc.Block())

        @block.sync
        def _(sp):
            x_rows = x.rearrange("b (t p) d -> p (b t) d", p=P)
            for c in range(halves):
                at = slice(c * tiles_half, (c + 1) * tiles_half)
                sp.dma_start(x_sb[:, at, :], x_rows[:, at, :]).then_inc(x_loaded[c], 16)

            def load_attention(L, kind):
                k_rows = P if kind == "self" else ctx_width
                wk, wv = (wk_self, wv_self) if kind == "self" else (wk_cross, wv_cross)
                n = att_n(L, kind)
                sp.wait_ge(wv_split, n * 2 + 1)
                sp.dma_start(wv_raw[0:k_rows, :], wv[bass.ds(L, 1)].rearrange("a p n -> (a p) n")
                             ).then_inc(wv_loaded, 16)
                sp.wait_ge(pair_split, n * pairs + 1)
                sp.dma_start(wq_raw[:], wq[bass.ds(n, 1)].rearrange("a p n -> (a p) n")
                             ).then_inc(wqk_loaded, 16)
                sp.dma_start(wk_raw[0:k_rows, :], wk[bass.ds(L, 1)].rearrange("a p n -> (a p) n")
                             ).then_inc(wqk_loaded, 16)
                sp.wait_ge(wo_used, n * halves + 1)
                sp.dma_start(wo_sb[:], wo[bass.ds(n, 1)].rearrange("a (i p) n -> p (a i) n", p=P)
                             ).then_inc(wo_loaded, 16)

            def copy_values(L, kind):
                n = att_n(L, kind)

                def copy_half(i, c, weighed):
                    sp.wait_ge(pv_made, weighed)
                    at = half_tiles(c)
                    at = slice(at[0], at[-1] + 1)
                    sp.dma_start(v_pair[:, at, :], v_sb[:, at, bass.ds(i * P, P)]).then_inc(v_pair_copied[c], 16)

                first = pair_n(L, kind, 0) * batches + 1
                sp.wait_ge(*v_out_by(n, v_chunks // 2 - 1))
                copy_half(0, 0, first)
                sp.wait_ge(*v_out_by(n, v_chunks - 1))
                sp.wait_ge(*v_out_by(n, v_chunks - 2))
                copy_half(0, 1, first)
                with sp.Fori(1, pairs) as i:
                    done = pair_n(L, kind, i) * batches + 1
                    copy_half(i, 0, done - batches // 2)
                    copy_half(i, 1, done)

            with sp.Fori(0, layers) as L:
                load_attention(L, "self")
                sp.wait_ge(w_up_split, L + 1)
                sp.dma_start(w_up_raw[:], w_up[bass.ds(L, 1)].rearrange("a p n -> (a p) n")
                             ).then_inc(w_up_loaded, 16)
                sp.wait_ge(w_down_used, L * halves + 1)
                sp.dma_start(w_down_sb[:], w_down[bass.ds(L, 1)].rearrange("a (f p) n -> p (a f) n", p=P)
                             ).then_inc(w_down_loaded, 16)
                copy_values(L, "self")
                load_attention(L, "cross")
                copy_values(L, "cross")

            out_rows = out.rearrange("b (t p) d -> p (b t) d", p=P)
            for c in range(halves):
                at = slice(c * tiles_half, (c + 1) * tiles_half)
                sp.wait_ge(residual_done, (layers * 3 - 1) * halves + c + 1)
                sp.dma_start(out_rows[:, at, :], x_sb[:, at, :]).then_inc(out_stored[c], 16)
            for c in range(halves):
                sp.wait_ge(out_stored[c], 16)

        @block.gpsimd
        def _(pool):
            for k, credit in enumerate((wv_split, pair_split, w_up_split)):
                pool.memset(credits[:, k:k + 1], 0.0).then_inc(credit, 1)
            pool.memset(ident[:], 0.0).then_inc(zeroed, 1)
            pool.wait_ge(zeroed, 1)
            pool.affine_select(out=ident[:], in_=ident[:], compare_op=ALU.not_equal, fill=1.0, base=0,
                               pattern=[[-1, P]], channel_multiplier=1).then_inc(ident_ready, 1)
            pool.dma_start(rows_all[:], rows.rearrange("a n -> (a n)").partition_broadcast(P)
                           ).then_inc(rows_loaded, 16)

            def split(hi, lo, raw, link, done):
                pool.tensor_copy(hi, raw).then_inc(pool_link, 1)
                pool.wait_ge(pool_link, link)
                return pool.tensor_tensor(lo, raw, hi.bitcast(F32), ALU.subtract).then_inc(done, 1)

            links_att = 2 + 2 * pairs
            links_layer = 2 * links_att + 1

            def split_pair(L, kind, i):
                k_rows = P if kind == "self" else ctx_width
                link = L * links_layer + (ATT[kind] * links_att + 2) + i * 2
                pool.wait_ge(qk_made, pair_n(L, kind, i) * 4 + 1)
                pool.sem_inc(pool_held, 1)
                at = bass.ds(i * P, P)
                pool.tensor_copy(wp_hi[:, 0, :], wq_raw[:, at]).then_inc(pool_link, 1)
                pool.tensor_copy(wp_hi[0:k_rows, 1, :], wk_raw[0:k_rows, at]).then_inc(pool_link, 1)
                pool.wait_ge(pool_link, link + 2)
                pool.sem_inc(pool_held, 1)
                pool.tensor_tensor(wp_lo[:, 0, :], wq_raw[:, at], wp_hi[:, 0, :].bitcast(F32), ALU.subtract)
                pool.tensor_tensor(wp_lo[0:k_rows, 1, :], wk_raw[0:k_rows, at],
                                   wp_hi[0:k_rows, 1, :].bitcast(F32), ALU.subtract).then_inc(pair_split, 1)

            def add_row(L, kind, c):
                pool.wait_ge(ln_link, ln_n(L, kind, c) * LN_LINKS + LN_LINKS)
                pool.sem_inc(pool_held, 1)
                row = rows_all[:, bass.ds(L * (3 * width) + ROW[kind] * width, width)]
                for t in half_tiles(c):
                    last = pool.tensor_tensor(x_sb[:, t, :], x_sb[:, t, :], row, ALU.add)
                last.then_inc(row_added, 1)

            def normalise(n):
                for u in norm_by_pool:
                    pool.wait_ge(inverted, n * units + (u + 1))
                    pool.tensor_tensor(probs[:, u % 4], probs[:, u % 4],
                                       inv_sum[:, u % 4, :, None].broadcast_to([P, seq_tiles, seq]),
                                       ALU.mult).then_inc(normed_pool, 1)

            def attention(L, kind):
                k_rows = P if kind == "self" else ctx_width
                n = att_n(L, kind)
                pool.wait_ge(wv_loaded, (n + 1) * 16)
                pool.wait_ge(v_made, n * v_chunks + 1)
                pool.sem_inc(pool_held, 1)
                for part in range(2):
                    at = slice(part * 512, (part + 1) * 512)
                    split(wv_hi[0:k_rows, at], wv_lo[0:k_rows, at], wv_raw[0:k_rows, at],
                          L * links_layer + (ATT[kind] * links_att + part + 1), wv_split)
                pool.wait_ge(wqk_loaded, (n + 1) * 32)
                split_pair(L, kind, 0)
                for c in range(halves):
                    add_row(L, kind, c)
                with pool.Fori(0, pairs - 1) as i:
                    split_pair(L, kind, i + 1)
                    normalise(pair_n(L, kind, i))
                normalise(pair_n(L, kind, pairs - 1))

            pool.wait_ge(rows_loaded, 16)
            with pool.Fori(0, layers) as L:
                attention(L, "self")
                attention(L, "cross")
                pool.wait_ge(w_up_loaded, (L + 1) * 16)
                pool.wait_ge(w_down_used, L * halves + 1)
                pool.sem_inc(pool_held, 1)
                split(w_up_hi[:], w_up_lo[:], w_up_raw[:], (L + 1) * links_layer, w_up_split)
                for c in range(halves):
                    add_row(L, "mlp", c)
                    for f in range(gated_by_pool):
                        j = c * hidden_tiles + f
                        pool.wait_ge(up_out, L * (halves * gated_by_pool) + (c * gated_by_pool + f + 1))
                        pool.tensor_tensor(hidden_t[:, f, half_cols(c)], hidden_t[:, f, half_cols(c)],
                                           gate[:, j % 4, :], ALU.mult).then_inc(hidden_done_pool, 1)

        @block.tensor
        def _(pe):
            def product(out_ap, st, mv):
                nc.tensor.matmul(out_ap, st[1], mv[0], start=True, stop=False)
                nc.tensor.matmul(out_ap, st[0], mv[1], start=False, stop=False)
                return nc.tensor.matmul(out_ap, st[0], mv[0], start=False, stop=True)

            def turn_norm(L, kind, c):
                pe.wait_ge(ln_link, ln_n(L, kind, c) * LN_LINKS + LN_LINKS)
                for j, t in enumerate(half_tiles(c)):
                    last = nc.tensor.transpose(pv_bank[c][:, j * P:(j + 1) * P], xn[:, t, :], ident[:])
                last.then_inc(ln_turned, 1)

            def project_v(L, kind, chunks):
                k_rows, s_hi, s_lo = (P, h_hi, h_lo) if kind == "self" else (ctx_width, ctx_hi, ctx_lo)
                n = att_n(L, kind)
                for j in chunks:
                    t, to = v_chunk(j)
                    if j == 0 or j == tiles_half:
                        pe.wait_ge(wv_split, n * 2 + (2 + j // tiles_half))
                    ago = 3 if j < v_chunks // 2 else 2
                    if j >= ago:
                        pe.wait_ge(*v_out_by(n, j - ago))
                    at = slice(t * P, (t + 1) * P)
                    product(v_bank(j)[:],
                            (s_hi[0:k_rows, at], s_lo[0:k_rows, at]),
                            (wv_hi[0:k_rows, to], wv_lo[0:k_rows, to])).then_inc(v_made, 1)

            def project_qk(kind, which, c, to_bank):
                k_rows, s_hi, s_lo = (P, h_hi, h_lo) if which == 0 or kind == "self" else (ctx_width, ctx_hi, ctx_lo)
                at = half_cols(c)
                product(proj_bank[to_bank][:],
                        (wp_hi[0:k_rows, which, :], wp_lo[0:k_rows, which, :]),
                        (s_hi[0:k_rows, at], s_lo[0:k_rows, at])).then_inc(qk_made, 1)

            def score(n, u, has_prev):
                b, hh = u // 2, u % 2
                if u == 0:
                    pe.wait_ge(qk_lo_out, n * 4 + 2)
                if u == units // 2:
                    pe.wait_ge(qk_lo_out, n * 4 + 4)
                if u >= 2 or has_prev:
                    pe.wait_ge(exped, n * units + (u - 1))
                head = slice(hh * head_dim, (hh + 1) * head_dim)
                keys = slice(b * seq, (b + 1) * seq)
                for s in range(seq_tiles):
                    qs = slice(b * seq + s * P, b * seq + (s + 1) * P)
                    m = product(score_bank[u % 2][:, s * seq:(s + 1) * seq],
                                (qk_hi[0][head, qs], qk_lo[0][head, qs]),
                                (qk_hi[1][head, keys], qk_lo[1][head, keys]))
                m.then_inc(scored, 1)

            def turn(n, u, has_prev=True):
                pe.wait_ge(*normed_by(n, u))
                if u >= 2:
                    pe.wait_ge(*turned_out_by(n, u - 2))
                elif u == 0 and has_prev:
                    pe.wait_ge(*turned_out_by(n - 1, units - 2))
                for kt in range(seq_tiles):
                    for s in range(seq_tiles):
                        m = nc.tensor.transpose(
                            turn_bank[u % 2][:, kt * seq + s * P:kt * seq + (s + 1) * P],
                            probs[:, u % 4, s, kt * P:(kt + 1) * P], ident[:])
                m.then_inc(turned, 1)

            def weigh(n, b):
                if b % 2 == 0:
                    pe.wait_ge(v_pair_copied[b // 2], (n + 1) * 16)
                if b >= 2:
                    pe.wait_ge(heads_out_done, n * batches + (b - 1))
                if not (2 * b in by_act and 2 * b + 1 in by_act):
                    pe.wait_ge(*turned_out_by(n, 2 * b))
                pe.wait_ge(*turned_out_by(n, 2 * b + 1))
                for kt in range(seq_tiles):
                    for hh in range(2):
                        head = slice(hh * head_dim, (hh + 1) * head_dim)
                        m = nc.tensor.matmul(pv_bank[b % 2][head, 0:seq],
                                             v_pair[:, b * seq_tiles + kt, head],
                                             probs_t[:, (2 * b + hh) % 4, kt, :],
                                             start=(kt == 0), stop=(kt == seq_tiles - 1))
                m.then_inc(pv_made, 1)

            def pair_body(L, kind, i, has_prev, has_next):
                n = pair_n(L, kind, i)
                score(n, 0, has_prev)
                if has_prev:
                    project_qk(kind, 0, 1, 0)
                    turn(n - 1, 5)
                else:
                    if kind == "self":
                        pe.wait_ge(h_ready, ln_n(L, kind, 1) + 1)
                    project_v(L, kind, range(v_chunks // 2, v_chunks // 2 + 4))
                    pe.wait_ge(h_ready, ln_n(L, kind, 1) + 1)
                    project_qk(kind, 0, 1, 0)
                score(n, 1, has_prev)
                project_qk(kind, 1, 1, 1)
                if has_prev:
                    turn(n - 1, 6)
                else:
                    project_v(L, kind, range(v_chunks // 2 + 4, v_chunks - 2))
                score(n, 2, has_prev)
                if has_prev:
                    turn(n - 1, 7)
                    weigh(n - 1, 2)
                else:
                    project_v(L, kind, range(v_chunks - 2, v_chunks))
                score(n, 3, has_prev)
                if not has_prev:
                    pe.wait_ge(*v_out_by(att_n(L, kind), v_chunks - 2))
                    pe.wait_ge(*v_out_by(att_n(L, kind), v_chunks - 1))
                turn(n, 0, has_prev)
                if has_prev:
                    weigh(n - 1, 3)
                score(n, 4, has_prev)
                if has_next:
                    pe.wait_ge(pair_split, n + 3)
                    project_qk(kind, 0, 0, 0)
                turn(n, 1)
                score(n, 5, has_prev)
                if has_next:
                    project_qk(kind, 1, 0, 1)
                turn(n, 2)
                score(n, 6, has_prev)
                turn(n, 3)
                weigh(n, 0)
                score(n, 7, has_prev)
                turn(n, 4)
                weigh(n, 1)

            def last_units(L, kind, then):
                n = pair_n(L, kind, pairs - 1)
                turn(n, 5)
                project_out(L, kind, 0, (0, 1))
                turn(n, 6)
                weigh(n, 2)
                turn(n, 7)
                project_out(L, kind, 0, (2, 3))
                weigh(n, 3)
                project_out(L, kind, 1, (4, 5))
                project_out(L, kind, 1, (6,))
                turn_norm(L, then, 0)
                project_out(L, kind, 1, (7,))

            def project_out(L, kind, c, some_tiles):
                if some_tiles[0] % tiles_half == 0:
                    pe.wait_ge(wo_loaded, (att_n(L, kind) + 1) * 16)
                    pe.wait_ge(exped, pair_n(L, kind, pairs - 1) * units + (units - 1 + c))
                done = some_tiles[-1] // seq_tiles + 1
                pe.wait_ge(heads_out_done, (pair_n(L, kind, pairs - 1)) * batches + done)
                for t in some_tiles:
                    j = t % tiles_half
                    for i in range(pairs):
                        m = nc.tensor.matmul(score_bank[c][:, j * P:(j + 1) * P],
                                             heads_t[:, i, t * P:(t + 1) * P], wo_sb[:, i, :],
                                             start=(i == 0), stop=(i == pairs - 1))
                if some_tiles[-1] % tiles_half == tiles_half - 1:
                    m.then_inc(wo_used, 1)

            def attention(L, kind):
                n = att_n(L, kind)
                if kind == "self":
                    pe.wait_ge(h_ready, ln_n(L, kind, 0) + 1)
                project_v(L, kind, range(0, v_chunks // 2 - 2))
                pe.wait_ge(pair_split, n * pairs + 2)
                pe.wait_ge(h_ready, ln_n(L, kind, 0) + 1)
                project_qk(kind, 0, 0, 0)
                project_qk(kind, 1, 0, 1)
                project_v(L, kind, range(v_chunks // 2 - 2, v_chunks // 2))
                pe.wait_ge(*v_out_by(n, 5))
                turn_norm(L, kind, 1)
                pair_body(L, kind, 0, False, True)
                pe.sem_inc(pe_held, 1)
                with pe.Fori(1, pairs - 1) as i:
                    pair_body(L, kind, i, True, True)
                pair_body(L, kind, pairs - 1, True, False)
                last_units(L, kind, "cross" if kind == "self" else "mlp")

            def project_up(L, c):
                n = L * (halves * hidden_tiles)
                pe.wait_ge(h_ready, ln_n(L, "mlp", c) + 1)
                for f in range(hidden_tiles):
                    j = c * hidden_tiles + f
                    for which, to in ((1, score_bank[j % 2]), (0, up_bank[j % 4])):
                        if which == 1 and c == 0 and f < 2:
                            pe.wait_ge(residual_done, L * (3 * halves) + halves + f + 1)
                        elif which == 1:
                            pe.wait_ge(gate_done, n + j - 1)
                        elif j >= 4:
                            if f < gated_by_pool:
                                pe.wait_ge(up_out, L * (halves * gated_by_pool) + (f + 1))
                            else:
                                pe.wait_ge(*gated_by(L, j - 4))
                        at = slice(which * hidden + f * P, which * hidden + (f + 1) * P)
                        product(to[:], (w_up_hi[:, at], w_up_lo[:, at]),
                                (h_hi[:, half_cols(c)], h_lo[:, half_cols(c)])
                                ).then_inc((up_made, gate_made)[which], 1)

            def project_down(L, c, some_tiles):
                if some_tiles[0] % tiles_half == 0:
                    pe.wait_ge(*gated_by(L, c * hidden_tiles + gated_by_pool - 1))
                    pe.wait_ge(*gated_by(L, (c + 1) * hidden_tiles - 1))
                for t in some_tiles:
                    j = t % tiles_half
                    for f in range(hidden_tiles):
                        m = nc.tensor.matmul(pv_bank[c][:, j * P:(j + 1) * P],
                                             hidden_t[:, f, t * P:(t + 1) * P], w_down_sb[:, f, :],
                                             start=(f == 0), stop=(f == hidden_tiles - 1))
                if some_tiles[-1] % tiles_half == tiles_half - 1:
                    m.then_inc(w_down_used, 1)

            def mlp(L):
                pe.wait_ge(w_up_split, L + 2)
                project_up(L, 0)
                turn_norm(L, "mlp", 1)
                pe.wait_ge(w_down_loaded, (L + 1) * 16)
                project_down(L, 0, half_tiles(0))
                project_up(L, 1)
                project_down(L, 1, (4, 5))
                turn_norm(L + 1, "self", 0)
                project_down(L, 1, (6, 7))

            pe.wait_ge(ident_ready, 1)
            for credit in (v_made, qk_made, wo_used, w_down_used, pv_made):
                nc.tensor.transpose(pv_bank[0][:, 0:P], ident[:], ident[:]).then_inc(credit, 1)
            pe.wait_ge(ctx_loaded, 16)
            for c in range(halves):
                for j, t in enumerate(half_tiles(c)):
                    m = nc.tensor.transpose(turn_bank[c][0:ctx_width, j * P:(j + 1) * P],
                                            ctx_rows[:, t, :], ident[:])
                m.then_inc(ctx_turned, 1)
            turn_norm(0, "self", 0)
            pe.wait_ge(ctx_ready, halves)
            with pe.Fori(0, layers) as L:
                attention(L, "self")
                attention(L, "cross")
                mlp(L)

        @block.scalar
        def _(act):
            def load_table(func):
                nc.scalar.activation(table_scratch[:], cols[:, 0:1], func)

            def norm_full(L, kind, c):
                act.wait_ge(ln_turned, ln_n(L, kind, c) + 1)
                act.sem_inc(act_held, 1)
                for h in (h_hi, h_full):
                    m = nc.scalar.activation(h[:, half_cols(c)], pv_bank[c][:], ACT.Identity,
                                             bias=cols[:, bass.ds(L * n_cols + (G[kind] + 1), 1)],
                                             scale=cols[:, bass.ds(L * n_cols + G[kind], 1)])
                m.then_inc(h_full_ready, 1)

            def v_out(L, kind, chunks):
                n = att_n(L, kind)
                for j in chunks:
                    if j not in v_by_act:
                        continue
                    act.wait_ge(v_made, n * v_chunks + j + 2)
                    nc.scalar.activation(v_part(j), v_bank(j)[:], ACT.Copy).then_inc(v_out_act, 1)

            def qk_high(n, j, which, c, from_bank):
                act.wait_ge(qk_made, n * 4 + j + 2)
                nc.scalar.activation(qk_hi[which][:, half_cols(c)], proj_bank[from_bank][:], ACT.Copy,
                                     scale=(scale, 1.0)[which]).then_inc(qk_hi_out, 1)

            def exponentials(n, u):
                act.wait_ge(maxed, n * units + u + 1)
                for s in range(seq_tiles):
                    m = nc.scalar.activation(probs[:, u % 4, s, :], score_bank[u % 2][:, s * seq:(s + 1) * seq],
                                             ACT.Exp, bias=neg_max[:, u % 4, s:s + 1],
                                             accum_out=row_sum[:, u % 4, s:s + 1])
                m.then_inc(exped, 1)

            def turned_out(n, u):
                act.wait_ge(turned, n * units + (u + 1))
                nc.scalar.activation(probs_t[:, u % 4, :, :].rearrange("p a b -> p (a b)"),
                                     turn_bank[u % 2][:], ACT.Copy).then_inc(turned_out_act, 1)

            def heads_t_out(n, i, b):
                act.wait_ge(pv_made, n * batches + (b + 2))
                act.sem_inc(act_held, 1)
                nc.scalar.activation(heads_t[:, bass.ds(i, 1), b * seq:(b + 1) * seq].rearrange("p a b -> p (a b)"),
                                     pv_bank[b % 2][:, 0:seq], ACT.Copy).then_inc(heads_out_done, 1)

            def pair_body(L, kind, i, has_prev, has_next):
                n = pair_n(L, kind, i)
                exponentials(n, 0)
                if has_prev:
                    qk_high(n, 2, 0, 1, 0)
                    turned_out(n - 1, 6)
                else:
                    v_out(L, kind, range(v_chunks // 2, v_chunks // 2 + 4))
                    qk_high(n, 2, 0, 1, 0)
                exponentials(n, 1)
                qk_high(n, 3, 1, 1, 1)
                if has_prev:
                    turned_out(n - 1, 7)
                else:
                    v_out(L, kind, range(v_chunks // 2 + 4, v_chunks - 2))
                exponentials(n, 2)
                if has_prev:
                    heads_t_out(n - 1, i - 1, 2)
                else:
                    v_out(L, kind, range(v_chunks - 2, v_chunks))
                turned_out(n, 0)
                exponentials(n, 3)
                if has_prev:
                    heads_t_out(n - 1, i - 1, 3)
                exponentials(n, 4)
                if has_next:
                    qk_high(n, 4, 0, 0, 0)
                turned_out(n, 2)
                exponentials(n, 5)
                if has_next:
                    qk_high(n, 5, 1, 0, 1)
                exponentials(n, 6)
                heads_t_out(n, i, 0)
                turned_out(n, 4)
                exponentials(n, 7)
                heads_t_out(n, i, 1)

            def attention(L, kind):
                n = pair_n(L, kind, 0)
                norm_full(L, kind, 0)
                v_out(L, kind, range(0, v_chunks // 2 - 2))
                qk_high(n, 0, 0, 0, 0)
                qk_high(n, 1, 1, 0, 1)
                v_out(L, kind, range(v_chunks // 2 - 2, v_chunks // 2))
                norm_full(L, kind, 1)
                pair_body(L, kind, 0, False, True)
                with act.Fori(1, pairs - 1) as i:
                    pair_body(L, kind, i, True, True)
                pair_body(L, kind, pairs - 1, True, False)
                last = pair_n(L, kind, pairs - 1)
                turned_out(last, 6)
                heads_t_out(last, pairs - 1, 2)
                turned_out(last, 7)
                heads_t_out(last, pairs - 1, 3)

            act.dma_start(ctx_rows[:], ctx.rearrange("b (t p) d -> p (b t) d", p=P)).then_inc(ctx_loaded, 16)
            act.dma_start(cols[:], columns).then_inc(cols_loaded, 16)
            for c in range(halves):
                act.wait_ge(ctx_turned, c + 1)
                nc.scalar.activation(ctx_hi[0:ctx_width, half_cols(c)], turn_bank[c][0:ctx_width, :],
                                     ACT.Copy).then_inc(ctx_hi_ready, 1)
            act.wait_ge(cols_loaded, 16)
            with act.Fori(0, layers) as L:
                attention(L, "self")
                attention(L, "cross")
                n = L * (halves * hidden_tiles)
                load_table(ACT.Gelu)
                norm_full(L, "mlp", 0)
                for j in range(halves * hidden_tiles):
                    c, f = j // hidden_tiles, j % hidden_tiles
                    if j == hidden_tiles:
                        norm_full(L, "mlp", 1)
                    act.wait_ge(gate_made, n + j + 1)
                    if j >= 4:
                        act.wait_ge(*gated_by(L, j - 4))
                    act.sem_inc(act_held, 1)
                    nc.scalar.activation(gate[:, j % 4, :], score_bank[j % 2][:], ACT.Gelu,
                                         bias=cols[:, bass.ds(L * n_cols + (B_UP + hidden_tiles + f), 1)]
                                         ).then_inc(gate_done, 1)
                    if f < gated_by_pool:
                        act.wait_ge(up_made, n + j + 1)
                        act.sem_inc(act_held, 1)
                        nc.scalar.activation(hidden_t[:, f, half_cols(c)], up_bank[j % 4][:], ACT.Identity,
                                             bias=cols[:, bass.ds(L * n_cols + (B_UP + f), 1)]
                                             ).then_inc(up_out, 1)
                load_table(ACT.Exp)

        @block.vector
        def _(dve):
            def norm_moments(L, kind, c):
                base = ln_n(L, kind, c) * LN_LINKS
                ts = half_tiles(c)
                h = slice(ts[0], ts[-1] + 1)
                for t in ts:
                    m = nc.vector.bn_stats(stats[:, t, :], x_sb[:, t, :])
                m.then_inc(ln_link, 1)
                dve.wait_ge(ln_link, base + 1)
                dve.sem_inc(dve_held, 1)
                for t in ts:
                    m = nc.vector.bn_aggr(mean_var[:, t, :], stats[:, t, :])
                m.then_inc(ln_link, 1)

            def norm_rstd(L, kind, c):
                base = ln_n(L, kind, c) * LN_LINKS
                ts = half_tiles(c)
                h = slice(ts[0], ts[-1] + 1)
                dve.wait_ge(ln_link, base + 2)
                nc.vector.tensor_scalar(half_var[:, h], mean_var[:, h, 1], -0.5, -0.5 * EPS, ALU.mult, ALU.add)
                nc.vector.tensor_scalar(var_eps[:, h], mean_var[:, h, 1], EPS, None, ALU.add).then_inc(ln_link, 1)
                dve.wait_ge(ln_link, base + 3)
                nc.vector.tensor_scalar(rstd[:, h].bitcast(I32), var_eps[:, h].bitcast(I32), -0.5, RSQRT_MAGIC,
                                        ALU.mult, ALU.add).then_inc(ln_link, 1)
                dve.wait_ge(ln_link, base + 4)
                nc.vector.tensor_tensor(half_root[:, h], rstd[:, h], half_var[:, h], ALU.mult).then_inc(ln_link, 1)
                for k in range(NEWTON_STEPS):
                    dve.wait_ge(ln_link, base + 5 + 2 * k)
                    nc.vector.tensor_tensor(newton[:, h], half_root[:, h], rstd[:, h], ALU.mult).then_inc(ln_link, 1)
                    dve.wait_ge(ln_link, base + 6 + 2 * k)
                    for factor in (half_root, rstd) if k < NEWTON_STEPS - 1 else (rstd,):
                        m = nc.vector.scalar_tensor_tensor(out=factor[:, h], in0=newton[:, h], scalar=1.5,
                                                           in1=factor[:, h], op0=ALU.add, op1=ALU.mult)
                    m.then_inc(ln_link, 1)

            def norm_scaled(L, kind, c):
                ts = half_tiles(c)
                dve.wait_ge(ln_link, ln_n(L, kind, c) * LN_LINKS + LN_LINKS - 1)
                for t in ts:
                    m = nc.vector.tensor_scalar(xn[:, t, :], x_sb[:, t, :], mean_var[:, t, 0:1], rstd[:, t:t + 1],
                                                ALU.subtract, ALU.mult)
                m.then_inc(ln_link, 1)

            def norm_rows(L, kind, c):
                norm_moments(L, kind, c)
                norm_rstd(L, kind, c)
                norm_scaled(L, kind, c)

            def norm_low(L, kind, c):
                n = ln_n(L, kind, c)
                at = half_cols(c)
                dve.wait_ge(h_full_ready, n + 1)
                nc.vector.tensor_tensor(h_lo[:, at], h_full[:, at], h_hi[:, at].bitcast(F32),
                                        ALU.subtract).then_inc(h_ready, 1)

            def residual(L, stage, c, from_bank):
                n = L * (3 * halves) + LN[stage] * halves + c
                dve.wait_ge(row_added, n + 1)
                at = half_tiles(c)
                rows_c = x_sb[:, at[0]:at[-1] + 1, :].rearrange("p t d -> p (t d)")
                nc.vector.tensor_tensor(rows_c, from_bank[:], rows_c, ALU.add).then_inc(residual_done, 1)
                return n + 1

            def v_out(L, kind, chunks):
                n = att_n(L, kind)
                for j in chunks:
                    if j not in v_by_dve:
                        continue
                    dve.wait_ge(v_made, n * v_chunks + j + 2)
                    nc.vector.tensor_copy(v_part(j), v_bank(j)[:]).then_inc(v_out_dve, 1)

            def qk_low(n, j, which, c, from_bank):
                dve.wait_ge(qk_hi_out, n * 4 + j + 1)
                nc.vector.scalar_tensor_tensor(out=qk_lo[which][:, half_cols(c)], in0=proj_bank[from_bank][:],
                                               scalar=(scale, 1.0)[which],
                                               in1=qk_hi[which][:, half_cols(c)].bitcast(F32),
                                               op0=ALU.mult, op1=ALU.subtract).then_inc(qk_lo_out, 1)

            def maxima(n, u):
                dve.wait_ge(scored, n * units + u + 1)
                nc.vector.tensor_reduce(neg_max[:, u % 4, :],
                                        score_bank[u % 2][:].rearrange("p (s k) -> p s k", k=seq),
                                        AX.X, ALU.max, negate=True).then_inc(maxed, 1)

            def turned_out(n, u):
                dve.wait_ge(turned, n * units + (u + 1))
                nc.vector.tensor_copy(probs_t[:, u % 4, :, :].rearrange("p a b -> p (a b)"),
                                      turn_bank[u % 2][:]).then_inc(turned_out_dve, 1)

            def normalise(n, u):
                dve.wait_ge(exped, n * units + (u + 1))
                nc.vector.reciprocal(inv_sum[:, u % 4, :], row_sum[:, u % 4, :]).then_inc(inverted, 1)
                if u in norm_by_pool:
                    return
                dve.wait_ge(inverted, n * units + (u + 1))
                for s in range(seq_tiles):
                    m = nc.vector.tensor_scalar(probs[:, u % 4, s, :], probs[:, u % 4, s, :],
                                                inv_sum[:, u % 4, s:s + 1], None, ALU.mult)
                m.then_inc(normed_dve, 1)

            def pair_body(L, kind, i, has_prev, has_next):
                n = pair_n(L, kind, i)
                maxima(n, 0)
                if has_prev:
                    normalise(n - 1, 7)
                    turned_out(n - 1, 5)
                elif kind == "self":
                    norm_low(L, kind, 1)
                    v_out(L, kind, range(v_chunks // 2, v_chunks // 2 + 4))
                else:
                    v_out(L, kind, range(v_chunks // 2, v_chunks // 2 + 2))
                    norm_low(L, kind, 1)
                    v_out(L, kind, range(v_chunks // 2 + 2, v_chunks // 2 + 4))
                maxima(n, 1)
                normalise(n, 0)
                qk_low(n, 2, 0, 1, 0)
                if not has_prev:
                    v_out(L, kind, range(v_chunks // 2 + 4, v_chunks - 2))
                maxima(n, 2)
                normalise(n, 1)
                qk_low(n, 3, 1, 1, 1)
                if not has_prev:
                    v_out(L, kind, range(v_chunks - 2, v_chunks))
                maxima(n, 3)
                normalise(n, 2)
                maxima(n, 4)
                normalise(n, 3)
                turned_out(n, 1)
                maxima(n, 5)
                if has_next:
                    qk_low(n, 4, 0, 0, 0)
                normalise(n, 4)
                maxima(n, 6)
                turned_out(n, 3)
                if has_next:
                    qk_low(n, 5, 1, 0, 1)
                normalise(n, 5)
                maxima(n, 7)
                normalise(n, 6)

            def attention(L, kind):
                n = pair_n(L, kind, 0)
                norm_low(L, kind, 0)
                if kind == "self":
                    norm_rows(L, kind, 1)
                else:
                    sum_then_norm(L, "self", "cross", 1)
                qk_low(n, 0, 0, 0, 0)
                qk_low(n, 1, 1, 0, 1)
                pair_body(L, kind, 0, False, True)
                with dve.Fori(1, pairs - 1) as i:
                    pair_body(L, kind, i, True, True)
                pair_body(L, kind, pairs - 1, True, False)
                last = pair_n(L, kind, pairs - 1)
                normalise(last, 7)
                turned_out(last, 5)

            def sum_then_norm(L, stage, then, c):
                dve.wait_ge(wo_used, att_n(L, stage) * halves + c + 2)
                done = residual(L, stage, c, score_bank[c])
                dve.wait_ge(residual_done, done)
                norm_rows(L, then, c)

            def gated(L, j):
                c, f = j // hidden_tiles, j % hidden_tiles
                n = L * (halves * hidden_tiles)
                dve.wait_ge(up_made, n + j + 1)
                dve.wait_ge(gate_done, n + j + 1)
                nc.vector.scalar_tensor_tensor(out=hidden_t[:, f, half_cols(c)], in0=up_bank[j % 4][:],
                                               scalar=cols[:, bass.ds(L * n_cols + (B_UP + f), 1)],
                                               in1=gate[:, j % 4, :],
                                               op0=ALU.add, op1=ALU.mult).then_inc(hidden_done_dve, 1)

            dve.wait_ge(x_loaded[0], 16)
            norm_rows(0, "self", 0)
            dve.wait_ge(x_loaded[1], 16)
            dve.wait_ge(cols_loaded, 16)
            for c in range(halves):
                at = half_cols(c)
                dve.wait_ge(ctx_hi_ready, c + 1)
                nc.vector.tensor_tensor(ctx_lo[0:ctx_width, at], turn_bank[c][0:ctx_width, :],
                                        ctx_hi[0:ctx_width, at].bitcast(F32), ALU.subtract).then_inc(ctx_ready, 1)
            with dve.Fori(0, layers) as L:
                attention(L, "self")
                sum_then_norm(L, "self", "cross", 0)
                attention(L, "cross")
                sum_then_norm(L, "cross", "mlp", 0)
                norm_low(L, "mlp", 0)
                sum_then_norm(L, "cross", "mlp", 1)
                for f in range(gated_by_pool, hidden_tiles):
                    gated(L, f)
                norm_low(L, "mlp", 1)
                dve.wait_ge(w_down_used, L * halves + 2)
                done = residual(L, "mlp", 0, pv_bank[0])
                dve.wait_ge(residual_done, done)
                norm_moments(L + 1, "self", 0)
                norm_rstd(L + 1, "self", 0)
                for f in range(gated_by_pool, hidden_tiles):
                    gated(L, hidden_tiles + f)
                norm_scaled(L + 1, "self", 0)
                dve.wait_ge(w_down_used, L * halves + 3)
                done = residual(L, "mlp", 1, pv_bank[1])
                dve.wait_ge(residual_done, done)


_NAMES = [
    {"wq": ("wq1", "wq2"), "wk": ("wk1", "wk2"), "wv": ("wv1", "wv2"), "wo": ("wo1", "wo2"),
     "bo": ("bo1", "bo2"), "g": ("g1", "g2", "g3"), "b": ("b1", "b2", "b3"),
     "w_up": "w_ff1", "b_up": "b_ff1", "w_down": "w_ff2", "b_down": "b_ff2"},
    {"wq": ("Wq1", "Wq2"), "wk": ("Wk1", "Wk2"), "wv": ("Wv1", "Wv2"), "wo": ("Wo1", "Wo2"),
     "bo": ("bo1", "bo2"), "g": ("g1", "g2", "g3"), "b": ("be1", "be2", "be3"),
     "w_up": "Wp", "b_up": "bp", "w_down": "W2", "b_down": "b2"},
]


def kernel(**inputs):
    import numpy as _np
    import concourse.bacc as _bacc
    from concourse import mybir as _mybir
    from concourse.bass_utils import run_bass_kernel_spmd as _run

    def layer(n, name):
        return _np.asarray(inputs[f"L{n}_xattn_{name}"])

    ls = range(len(_NAMES))
    columns, rows = [], []
    for n in ls:
        names = _NAMES[n]
        for g, b in zip(names["g"], names["b"]):
            columns += [layer(n, g), layer(n, b)]
        columns += list(layer(n, names["b_up"]).reshape(-1, 128))
        rows += [layer(n, names["bo"][0]), layer(n, names["bo"][1]), layer(n, names["b_down"])]
    arrays = {
        "x": _np.asarray(inputs["x"]),
        "ctx": _np.asarray(inputs["ctx_768"]),
        "wq": _np.stack([layer(n, m) for n in ls for m in _NAMES[n]["wq"]]),
        "wk_self": _np.stack([layer(n, _NAMES[n]["wk"][0]) for n in ls]),
        "wv_self": _np.stack([layer(n, _NAMES[n]["wv"][0]) for n in ls]),
        "wk_cross": _np.stack([layer(n, _NAMES[n]["wk"][1]) for n in ls]),
        "wv_cross": _np.stack([layer(n, _NAMES[n]["wv"][1]) for n in ls]),
        "wo": _np.stack([layer(n, m) for n in ls for m in _NAMES[n]["wo"]]),
        "w_up": _np.stack([layer(n, _NAMES[n]["w_up"]) for n in ls]),
        "w_down": _np.stack([layer(n, _NAMES[n]["w_down"]) for n in ls]),
        "columns": _np.stack(columns, axis=1),
        "rows": _np.stack(rows),
    }
    arrays = {f"in_{k}_dram": _np.ascontiguousarray(v) for k, v in arrays.items()}
    nc = _bacc.Bacc("TRN2", target_bir_lowering=False, num_devices=1)
    args = [nc.dram_tensor(k, v.shape, _mybir.dt.from_np(v.dtype), kind="ExternalInput").ap()
            for k, v in arrays.items()]
    out = nc.dram_tensor("out_0_dram", tuple(inputs["x"].shape), _mybir.dt.float32, kind="ExternalOutput").ap()
    transformer_kernel(nc, *args, out)
    r = _run(nc, [arrays], core_ids=[0])
    return r.results[0]["out_0_dram"]
```
